# Optimizing a Trainium2 kernel written in Bass

```python
import numpy as np
import jax
import jax.numpy as jnp

def _softmax(x, axis=-1):
    return jax.nn.softmax(x, axis=axis)

def _gelu(x):
    return jax.nn.gelu(x, approximate=True)

def _silu(x):
    return jax.nn.silu(x)

def _sigmoid(x):
    return jax.nn.sigmoid(x)

def _layernorm(x, axis=-1, eps=1e-05):
    m = jnp.mean(x, axis=axis, keepdims=True)
    v = jnp.var(x, axis=axis, keepdims=True)
    return (x - m) / jnp.sqrt(v + eps)

def _scatter_add(tgt, idx, src, axis=0):
    return tgt.at[idx].add(src)

def _segment_sum(src, seg, n):
    return jax.ops.segment_sum(src, seg, n)
kernel_name = 'mk_xattn_ffn_d2_seqx_r8_19fb0f'

def setup_inputs(seed: int=0):
    np.random.seed(seed)
    _w = jnp.asarray

    def _rec_inputs():
        import jax
        import jax.numpy as jnp
        _rk = jax.random.key(seed)
        x = -0.0003929 + 0.9999 * jax.random.normal(jax.random.fold_in(_rk, 1), (16, 128, 256), jnp.float32)
        _lenS = 128 - jax.random.randint(jax.random.fold_in(_rk, 7), (16,), 0, max(1, 128 // 4) + 1, jnp.int32)
        _lenS2 = 128 - jax.random.randint(jax.random.fold_in(_rk, 8), (16,), 0, max(1, 128 // 4) + 1, jnp.int32)
        _ctx_2048P = jax.random.normal(jax.random.fold_in(_rk, 11), (16, 16, 256), jnp.float32)
        _ctx_2048c = jax.random.dirichlet(jax.random.fold_in(_rk, 511), 0.3 * jnp.ones((16,), jnp.float32), (16, 128))
        _ctx_2048t = jnp.einsum('bsk,bkd->bsd', _ctx_2048c, _ctx_2048P)
        _ctx_2048t = _ctx_2048t * jax.lax.rsqrt(jnp.mean(jnp.square(_ctx_2048t)) + 1e-12) * 0.953939
        ctx_2048 = 2.81802e-05 + 1.00001 * (_ctx_2048t + 0.3 * jax.random.normal(jax.random.fold_in(_rk, 611), (16, 128, 256), jnp.float32))
        return (x, ctx_2048)
    x, ctx_2048 = _rec_inputs()

    def _L0_xattn_setup():
        import jax, jax.numpy as jnp
        import numpy as np
        HIDDEN = 256
        NUM_HEADS = 16
        HEAD_DIM = HIDDEN // NUM_HEADS
        CHUNK = 128
        SCALE = HEAD_DIM ** (-0.5)

        def _chunked_causal_attention(q, k, v):
            B, H, S, D = q.shape
            n_chunks = S // CHUNK
            kc = k.reshape(B, H, n_chunks, CHUNK, D).transpose(2, 0, 1, 3, 4)
            vc = v.reshape(B, H, n_chunks, CHUNK, D).transpose(2, 0, 1, 3, 4)
            j0s = jnp.arange(n_chunks) * CHUNK
            q_idx = jnp.arange(S)[:, None]
            k_off = jnp.arange(CHUNK)[None, :]
            out0 = jnp.zeros_like(q)
            m0 = jnp.full((B, H, S, 1), -jnp.inf, dtype=q.dtype)
            s0 = jnp.zeros((B, H, S, 1), dtype=q.dtype)

            def step(carry, inputs):
                out, m, s = carry
                kj, vj, j0 = inputs
                scores = jnp.einsum('bhqd,bhkd->bhqk', q, kj) * SCALE
                causal = j0 + k_off > q_idx
                scores = jnp.where(causal[None, None], -jnp.inf, scores)
                chunk_max = scores.max(axis=-1, keepdims=True)
                new_m = jnp.maximum(m, chunk_max)
                exp_old = jnp.exp(m - new_m)
                exp_c = jnp.exp(scores - new_m)
                new_s = s * exp_old + exp_c.sum(axis=-1, keepdims=True)
                out = out * (s / new_s) * exp_old + jnp.einsum('bhqk,bhkd->bhqd', exp_c / new_s, vj)
                return ((out, new_m, new_s), None)
            (out, _, _), _ = jax.lax.scan(step, (out0, m0, s0), (kc, vc, j0s))
            return out
        key = jax.random.key(seed)
        kq, kk, kv = jax.random.split(key, 3)
        B, S = (2, 512)
        return {'query': jax.random.normal(kq, (B, S, HIDDEN), dtype=jnp.float32), 'key': jax.random.normal(kk, (B, S, HIDDEN), dtype=jnp.float32), 'value': jax.random.normal(kv, (B, S, HIDDEN), dtype=jnp.float32)}
    _L0_xattn_all = _L0_xattn_setup()
    _L0_xattn_in = {k: v for k, v in _L0_xattn_all.items() if k in ()}
    del _L0_xattn_all

    def _L0_ffn_setup():
        import jax, jax.numpy as jnp
        import numpy as np
        B, S, D_IN, D_OUT, E, R = (4, 256, 256, 256, 8, 16)
        SCALING = 32.0 / 16.0
        key = jax.random.key(seed)
        ks = jax.random.split(key, 7)
        return {'x': jax.random.normal(ks[0], (B, S, D_IN), jnp.float32), 'base_w': jax.random.normal(ks[1], (D_OUT, D_IN), jnp.float32) * 0.02, 'base_b': jax.random.normal(ks[2], (D_OUT,), jnp.float32) * 0.02, 'router_w': jax.random.normal(ks[3], (E, D_IN), jnp.float32) * 0.02, 'router_b': jax.random.normal(ks[4], (E,), jnp.float32) * 0.02, 'lora_A': jax.random.normal(ks[5], (E, D_IN, R), jnp.float32) * 0.02, 'lora_B': jax.random.normal(ks[6], (E, R, D_OUT), jnp.float32) * 0.02}
    _L0_ffn_all = _L0_ffn_setup()
    _L0_ffn_in = {k: v for k, v in _L0_ffn_all.items() if k in ('base_w', 'base_b', 'router_w', 'router_b', 'lora_A', 'lora_B')}
    del _L0_ffn_all

    def _L1_xattn_setup():
        import jax, jax.numpy as jnp
        import numpy as np
        N_HEAD = 8
        key = jax.random.key(seed)
        k1, k2, k3 = jax.random.split(key, 3)
        B, D, L = (4, 128, 256)
        q = jax.random.normal(k1, (B, D, L), dtype=jnp.float32)
        k = jax.random.normal(k2, (B, D, L), dtype=jnp.float32)
        v = jax.random.normal(k3, (B, D, L), dtype=jnp.float32)
        gamma = jnp.ones((), dtype=jnp.float32)
        return {'q': q, 'k': k, 'v': v, 'gamma': gamma}
    _L1_xattn_all = _L1_xattn_setup()
    _L1_xattn_in = {k: v for k, v in _L1_xattn_all.items() if k in ('gamma',)}
    del _L1_xattn_all

    def _L1_ffn_setup():
        import jax, jax.numpy as jnp
        import numpy as np
        DIM = 256
        HIDDEN = 1024
        EPS = 1e-06

        def rms_norm(x, gamma):
            var = jnp.mean(x * x, axis=-1, keepdims=True)
            return x * jax.lax.rsqrt(var + EPS) * gamma

        def activation_quant(x):
            scale = 127.0 / jnp.maximum(jnp.max(jnp.abs(x), axis=-1, keepdims=True), 1e-05)
            return jnp.clip(jnp.round(x * scale), -128.0, 127.0) / scale

        def weight_quant(w):
            scale = 1.0 / jnp.maximum(jnp.mean(jnp.abs(w)), 1e-05)
            return jnp.clip(jnp.round(w * scale), -1.0, 1.0) / scale

        def bit_linear(x, w):
            xq = x + jax.lax.stop_gradient(activation_quant(x) - x)
            wq = w + jax.lax.stop_gradient(weight_quant(w) - w)
            return jnp.einsum('bsi,oi->bso', xq, wq)
        key = jax.random.key(seed)
        k_x, k_w1, k_w2 = jax.random.split(key, 3)
        x = jax.random.normal(k_x, (4, 256, DIM), dtype=jnp.float32)
        b1 = 1.0 / np.sqrt(DIM)
        b2 = 1.0 / np.sqrt(HIDDEN)
        w1 = jax.random.uniform(k_w1, (HIDDEN, DIM), dtype=jnp.float32, minval=-b1, maxval=b1)
        w2 = jax.random.uniform(k_w2, (DIM, HIDDEN), dtype=jnp.float32, minval=-b2, maxval=b2)
        gamma = jnp.ones((DIM,), dtype=jnp.float32)
        return {'x': x, 'w1': w1, 'w2': w2, 'gamma': gamma}
    _L1_ffn_all = _L1_ffn_setup()
    _L1_ffn_in = {k: v for k, v in _L1_ffn_all.items() if k in ('w1', 'w2', 'gamma')}
    del _L1_ffn_all
    return {'x': x, 'ctx_2048': ctx_2048, 'L0_ffn_base_w': _L0_ffn_in['base_w'], 'L0_ffn_base_b': _L0_ffn_in['base_b'], 'L0_ffn_router_w': _L0_ffn_in['router_w'], 'L0_ffn_router_b': _L0_ffn_in['router_b'], 'L0_ffn_lora_A': _L0_ffn_in['lora_A'], 'L0_ffn_lora_B': _L0_ffn_in['lora_B'], 'L1_xattn_gamma': _L1_xattn_in['gamma'], 'L1_ffn_w1': _L1_ffn_in['w1'], 'L1_ffn_w2': _L1_ffn_in['w2'], 'L1_ffn_gamma': _L1_ffn_in['gamma']}

def reference(x, ctx_2048, L0_ffn_base_w, L0_ffn_base_b, L0_ffn_router_w, L0_ffn_router_b, L0_ffn_lora_A, L0_ffn_lora_B, L1_xattn_gamma, L1_ffn_w1, L1_ffn_w2, L1_ffn_gamma):
    import jax
    import jax.numpy as jnp

    def _L0_xattn_ref(query, key, value):
        import jax, jax.numpy as jnp
        import numpy as np
        HIDDEN = 256
        NUM_HEADS = 16
        HEAD_DIM = HIDDEN // NUM_HEADS
        CHUNK = 128
        SCALE = HEAD_DIM ** (-0.5)

        def _chunked_causal_attention(q, k, v):
            B, H, S, D = q.shape
            n_chunks = S // CHUNK
            kc = k.reshape(B, H, n_chunks, CHUNK, D).transpose(2, 0, 1, 3, 4)
            vc = v.reshape(B, H, n_chunks, CHUNK, D).transpose(2, 0, 1, 3, 4)
            j0s = jnp.arange(n_chunks) * CHUNK
            q_idx = jnp.arange(S)[:, None]
            k_off = jnp.arange(CHUNK)[None, :]
            out0 = jnp.zeros_like(q)
            m0 = jnp.full((B, H, S, 1), -jnp.inf, dtype=q.dtype)
            s0 = jnp.zeros((B, H, S, 1), dtype=q.dtype)

            def step(carry, inputs):
                out, m, s = carry
                kj, vj, j0 = inputs
                scores = jnp.einsum('bhqd,bhkd->bhqk', q, kj) * SCALE
                causal = j0 + k_off > q_idx
                scores = jnp.where(causal[None, None], -jnp.inf, scores)
                chunk_max = scores.max(axis=-1, keepdims=True)
                new_m = jnp.maximum(m, chunk_max)
                exp_old = jnp.exp(m - new_m)
                exp_c = jnp.exp(scores - new_m)
                new_s = s * exp_old + exp_c.sum(axis=-1, keepdims=True)
                out = out * (s / new_s) * exp_old + jnp.einsum('bhqk,bhkd->bhqd', exp_c / new_s, vj)
                return ((out, new_m, new_s), None)
            (out, _, _), _ = jax.lax.scan(step, (out0, m0, s0), (kc, vc, j0s))
            return out
        B, S, _ = query.shape
        q = query.reshape(B, S, NUM_HEADS, HEAD_DIM).transpose(0, 2, 1, 3)
        k = key.reshape(B, S, NUM_HEADS, HEAD_DIM).transpose(0, 2, 1, 3)
        v = value.reshape(B, S, NUM_HEADS, HEAD_DIM).transpose(0, 2, 1, 3)
        out = _chunked_causal_attention(q, k, v)
        return out.transpose(0, 2, 1, 3).reshape(B, S, HIDDEN)

    def _L0_ffn_ref(x, base_w, base_b, router_w, router_b, lora_A, lora_B):
        import jax, jax.numpy as jnp
        import numpy as np
        B, S, D_IN, D_OUT, E, R = (4, 256, 256, 256, 8, 16)
        SCALING = 32.0 / 16.0
        b, s, d_in = x.shape
        n = b * s
        e = lora_A.shape[0]
        d_out = lora_B.shape[-1]
        result = jnp.einsum('bsd,od->bso', x, base_w) + base_b
        logits = jnp.einsum('bsd,ed->bse', x, router_w) + router_b
        probs = jax.nn.softmax(logits.astype(jnp.float32), axis=-1)
        top_vals, top_idx = jax.lax.top_k(probs, 2)
        top_vals = top_vals / jnp.sum(top_vals, axis=-1, keepdims=True)
        top_vals = top_vals.astype(x.dtype)
        flat_idx = top_idx.reshape(n, 2)
        flat_val = top_vals.reshape(n, 2)
        gate = jnp.zeros((n, e), x.dtype).at[jnp.arange(n)[:, None], flat_idx].set(flat_val)
        xf = x.reshape(n, d_in)
        mid = jnp.einsum('nd,edr->ner', xf, lora_A)
        mid = mid * gate[:, :, None]
        lora_out = jnp.einsum('ner,erd->nd', mid, lora_B)
        return result + SCALING * lora_out.reshape(b, s, d_out)

    def _L1_xattn_ref(q, k, v, gamma):
        import jax, jax.numpy as jnp
        import numpy as np
        N_HEAD = 8
        B, Dq, Lq = q.shape
        Dv, Lk = (v.shape[-2], v.shape[-1])
        h = N_HEAD
        dq = Dq // h
        dv = Dv // h
        qh = q.reshape(B, h, dq, Lq)
        kh = k.reshape(B, h, dq, Lk)
        vh = v.reshape(B, h, dv, Lk)
        scale = 1.0 / jnp.sqrt(jnp.asarray(dq, dtype=q.dtype))
        qk = jnp.einsum('bhdq,bhdl->bhql', qh, kh) * scale
        sm = jax.nn.softmax(qk, axis=-1)
        ret = jnp.einsum('bhql,bhdl->bhdq', sm, vh)
        ret = ret.reshape(B, Dv, Lq)
        return gamma * ret

    def _L1_ffn_ref(x, w1, w2, gamma):
        import jax, jax.numpy as jnp
        import numpy as np
        DIM = 256
        HIDDEN = 1024
        EPS = 1e-06

        def rms_norm(x, gamma):
            var = jnp.mean(x * x, axis=-1, keepdims=True)
            return x * jax.lax.rsqrt(var + EPS) * gamma

        def activation_quant(x):
            scale = 127.0 / jnp.maximum(jnp.max(jnp.abs(x), axis=-1, keepdims=True), 1e-05)
            return jnp.clip(jnp.round(x * scale), -128.0, 127.0) / scale

        def weight_quant(w):
            scale = 1.0 / jnp.maximum(jnp.mean(jnp.abs(w)), 1e-05)
            return jnp.clip(jnp.round(w * scale), -1.0, 1.0) / scale

        def bit_linear(x, w):
            xq = x + jax.lax.stop_gradient(activation_quant(x) - x)
            wq = w + jax.lax.stop_gradient(weight_quant(w) - w)
            return jnp.einsum('bsi,oi->bso', xq, wq)
        h = bit_linear(rms_norm(x, gamma), w1)
        h = jax.nn.gelu(h, approximate=False)
        return bit_linear(h, w2)
    x = x + _L0_xattn_ref(_layernorm(x, axis=-1), ctx_2048, ctx_2048)
    x = x + _L0_ffn_ref(_layernorm(x, axis=-1), L0_ffn_base_w, L0_ffn_base_b, L0_ffn_router_w, L0_ffn_router_b, L0_ffn_lora_A, L0_ffn_lora_B)
    x = x + _L1_xattn_ref(_layernorm(x, axis=-1), ctx_2048, ctx_2048, L1_xattn_gamma)
    x = x + _L1_ffn_ref(_layernorm(x, axis=-1), L1_ffn_w1, L1_ffn_w2, L1_ffn_gamma)
    return x

_drawn_inputs = setup_inputs


def setup_inputs(seed=0):
    import zlib

    import numpy as np

    out = dict(_drawn_inputs(seed))
    spreads = {'L1_ffn_gamma': (1.0, 0.6)}
    factors = {'L0_ffn_base_b': 2.681, 'L0_ffn_router_w': 2.673, 'L0_ffn_router_b': 8.0}
    for name, (base, spread) in spreads.items():
        noise = np.random.default_rng([zlib.crc32(name.encode()), seed]).standard_normal(out[name].shape)
        drawn = base * np.exp(spread * noise) if base else spread * noise
        out[name] = jnp.asarray(drawn.astype(out[name].dtype))
    for name, factor in factors.items():
        out[name] = (out[name] * factor).astype(out[name].dtype)
    return out
```

```python
from contextlib import ExitStack

import concourse.bass as bass
from concourse import mybir

F32 = mybir.dt.float32
BF16 = mybir.dt.bfloat16
U32 = mybir.dt.uint32
I32 = mybir.dt.int32
ALU = mybir.AluOpType
ACT = mybir.ActivationFunctionType
AX = mybir.AxisListType

NB = 16
P = 128
D = 256
DH = 16
H0 = D // DH
H1 = P // DH
FT = D // P
NE = 8
ER = 128
NFF = D + ER + NE
HID = 1024
HT = HID // P
PARTS = 3
RUN = PARTS * DH
STK = 6 * DH
STM = STK + 2
G = 4
LN_EPS = 1e-5
RMS_EPS = 1e-6
QEPS = 1e-5
SCALE = DH ** -0.5
MASKED = -1e30
ROUND = 12582912.0
LORA_SCALE = 2.0

Q_SINGLE = (0, 0, 1)
K_SINGLE = (0, 1, 0)

LOAD, PREP, SCORE0, MID, SCORE1, LATE = 3, 2, 1, 0, -1, -2
FIRST, LAST = -PREP, NB - 1 - LATE
W_ITERATIONS = (0, 1)
LOOP = (1 - LATE, NB - LOAD)

X_GROUPS = ((0, 1), (1, 2), (2, 4), (4, NB))

S_ORDER = [SCORE0] * (H0 // G) + [SCORE1] * H1
ST_ORDER = [MID] * (H0 // G) + [LATE] * H1
T_MAX1, T_MAX0, T_XH1, T_Q0, T_GATED, T_BACK = range(6)
T_ORDER = [LATE, SCORE0, MID, PREP, MID, LATE]
UT_ORDER = [MID, LATE]


def active(t, offset):
    return not isinstance(t, int) or 0 <= t + offset < NB


def ordinal(order, n, t):
    start = t if isinstance(t, int) else LOOP[0]
    before = sum(active(u, o) for u in range(FIRST, start) for o in order)
    here = sum(active(t, o) for o in order[:n])
    return before + here if isinstance(t, int) else (t - LOOP[0]) * len(order) + before + here


class Steps:

    def __init__(self, engine, sem, b, per):
        self.engine, self.sem, self.at = engine, sem, b * per

    def done(self, instruction):
        instruction.then_inc(self.sem, 1)
        self.at = self.at + 1
        return self

    def wait(self):
        self.engine.wait_ge(self.sem, self.at)


def head_column(h):
    return (h % H1) * FT + h // H1


def column_head(c):
    return (c % FT) * H1 + c // FT


def program(nc, x, kv, w_ff, base_b, router_b, lora_b, attn_gamma, w1, w2, mlp_gamma, out):
    with ExitStack() as ctx:
        def sb(name, shape, dt=F32):
            return ctx.enter_context(nc.sbuf_tensor(name, shape, dt))

        def bank(name, shape, dt=F32):
            return ctx.enter_context(nc.psum_tensor(name, shape, dt))

        def sem(name):
            return ctx.enter_context(nc.semaphore(name))

        k_parts = nc.dram_tensor("k_parts", [NB, 2, P, PARTS * D], BF16, kind="Internal").ap()
        q0_parts = nc.dram_tensor("q0_parts", [NB, P, PARTS * D], BF16, kind="Internal").ap()
        q1_parts = nc.dram_tensor("q1_parts", [NB, P, PARTS * D], BF16, kind="Internal").ap()

        ident = sb("ident", [P, P])
        ident_bf = sb("ident_bf", [P, P], BF16)
        mask_q = sb("mask_q", [P, G, P], BF16)
        mask_k = sb("mask_k", [P, G, P], BF16)
        iota8 = sb("iota8", [P, NE])
        iota8_i = sb("iota8_i", [P, NE], I32)
        neg_half = sb("neg_half", [P, 1])
        ones = sb("ones", [P, P])
        wff_sb = sb("wff_sb", [P, FT, NFF])
        lora_b_sb = sb("lora_b_sb", [ER, D])
        base_b_all = sb("base_b_all", [P, D])
        router_b_all = sb("router_b_all", [P, NE])
        attn_gamma_all = sb("attn_gamma_all", [P, 1])
        mlp_gamma_all = sb("mlp_gamma_all", [P, D])
        w1_sb = sb("w1_sb", [P, FT * HID])
        w2_sb = sb("w2_sb", [P, HT * D])
        w1_q = sb("w1_q", [P, FT, HID], BF16)
        w2_q = sb("w2_q", [P, HT, D], BF16)
        w_sum = sb("w_sum", [P, 2])
        w_mean = sb("w_mean", [P, 2])
        w_scale = sb("w_scale", [P, 2])
        round_all = sb("round_all", [P, 1])

        kv_in = sb("kv_in", [P, 2, D])
        v1_in = sb("v1_in", [P, D])
        k_split = sb("k_split", [P, 2, PARTS, D], BF16)
        k_rest = sb("k_rest", [P, 2, D])
        k0 = sb("k0", [STM, 2, H0 * P], BF16)
        k1 = sb("k1", [STM, 2, H1 * D], BF16)
        q0 = sb("q0", [STM, 2, H0 * P], BF16)
        q1 = sb("q1", [STM, 2, H1 * D], BF16)
        v0 = sb("v0", [P, 2, H0, 2 * DH])
        v1 = sb("v1", [P, FT * H1, 2 * DH])
        xs = sb("xs", [P, NB * D])
        stats0 = sb("stats0", [P, 6])
        stats1 = sb("stats1", [P, 6])
        stats2 = sb("stats2", [P, 6])
        mv0 = sb("mv0", [P, 2])
        mv1 = sb("mv1", [P, 2])
        mv2 = sb("mv2", [P, 2])
        var0 = sb("var0", [P, 1])
        var1 = sb("var1", [P, 1])
        var2 = sb("var2", [P, 1])
        rstd0 = sb("rstd0", [P, 1])
        rstd1 = sb("rstd1", [P, 1])
        rstd2 = sb("rstd2", [P, 1])
        xh0 = sb("xh0", [P, D])
        rest0 = sb("rest0", [P, D])
        q0_split = sb("q0_split", [P, PARTS, D], BF16)
        q0_t = sb("q0_t", [P, PARTS, D], BF16)
        xh2 = sb("xh2", [P, D])
        rest2 = sb("rest2", [P, D])
        q1_split = sb("q1_split", [P, PARTS, D], BF16)
        max0 = sb("max0", [P, H0])
        max0_split = sb("max0_split", [P, 2, H0], BF16)
        max0_t = sb("max0_t", [2 * H0, P], BF16)
        max1 = sb("max1", [P, FT, H1])
        max1_split = sb("max1_split", [P, FT, 2, H1], BF16)
        max1_t = sb("max1_t", [2 * H1, FT, P], BF16)
        p0 = sb("p0", [P, H0 // G, G * P])
        p1 = sb("p1", [P, H1, FT * D])
        u0 = sb("u0", [P, H0 // G, P])
        u1 = sb("u1", [P, H1 // G, D])
        rz0 = sb("rz0", [P, H0])
        rz1 = sb("rz1", [P, FT * H1])
        rzg1 = sb("rzg1", [P, FT * H1])
        a0 = sb("a0", [P, D])
        a1 = sb("a1", [P, FT, P])
        x1 = sb("x1", [P, D])
        x1b = sb("x1b", [P, D])
        xh1 = sb("xh1", [P, D])
        xh1_t = sb("xh1_t", [P, FT, P])
        logits = sb("logits", [P, NE])
        top = sb("top", [P, NE])
        top_i = sb("top_i", [P, NE], U32)
        top_if = sb("top_if", [P, 2])
        gap = sb("gap", [P, 1])
        e2 = sb("e2", [P, 1])
        esum = sb("esum", [P, 1])
        gate1 = sb("gate1", [P, 1])
        gate1s = sb("gate1s", [P, 1])
        gate2 = sb("gate2", [P, 1])
        pick1 = sb("pick1", [P, NE])
        pick2 = sb("pick2", [P, NE])
        gates = sb("gates", [P, NE])
        gated = sb("gated", [P, ER])
        gated_t = sb("gated_t", [ER, P])

        stats3 = sb("stats3", [P, 6])
        mv3 = sb("mv3", [P, 2])
        rms_in = sb("rms_in", [P, 1])
        rms = sb("rms", [P, 1])
        xn = sb("xn", [P, D])
        amax = sb("amax", [P, 2])
        amax_c = sb("amax_c", [P, 2])
        arec = sb("arec", [P, 2])
        qscale = sb("qscale", [P, 2])
        dequant = sb("dequant", [P, 2])
        xr = sb("xr", [P, D])
        xq = sb("xq", [P, D], BF16)
        xq_t = sb("xq_t", [P, FT, P], BF16)
        hid = sb("hid", [P, HID])
        hr = sb("hr", [P, HID])
        hq = sb("hq", [P, HID], BF16)
        hq_t = sb("hq_t", [P, HT, P], BF16)
        y = sb("y", [P, D])

        ps_s = [bank(f"ps_s{i}", [P, G * P]) for i in range(2)]
        ps_st = [bank(f"ps_st{i}", [P, G * P]) for i in range(2)]
        ps_u = bank("ps_u", [P, 512])
        ps_t = bank("ps_t", [P, 512])
        ps_ff = bank("ps_ff", [P, 512])
        ps_ut = bank("ps_ut", [P, 512])
        ps_t_bf = ps_t[:, :].bitcast(BF16)
        ps_t_h = ps_t_bf.rearrange("p (n q) -> p n q", q=P)
        ps_ut_bf = ps_ut[:, :].bitcast(BF16).rearrange("p (n q) -> p n q", q=P)

        consts_ready = sem("consts_ready")
        iota_ready = sem("iota_ready")
        masks_zeroed = sem("masks_zeroed")
        waited = sem("waited")
        weights_in = sem("weights_in")
        mlp_weights_in = sem("mlp_weights_in")
        kv_landed = sem("kv_landed")
        k_split_step = sem("k_split_step")
        k_parts_out = sem("k_parts_out")
        k0_landed = sem("k0_landed")
        k1_landed = sem("k1_landed")
        x_landed = [sem(f"x_landed{i}") for i in range(len(X_GROUPS))]
        v1_landed = sem("v1_landed")
        v0_placed = sem("v0_placed")
        v1_placed = sem("v1_placed")
        ln0_step = sem("ln0_step")
        ln1_step = sem("ln1_step")
        ln2_step = sem("ln2_step")
        rstd0_step = sem("rstd0_step")
        rstd1_step = sem("rstd1_step")
        rstd2_step = sem("rstd2_step")
        q0_turned = sem("q0_turned")
        q0_parts_out = sem("q0_parts_out")
        q0_landed = sem("q0_landed")
        q1_parts_out = sem("q1_parts_out")
        q1_landed = sem("q1_landed")
        s_ready = sem("s_ready")
        s_reduced = sem("s_reduced")
        st_ready = sem("st_ready")
        st_exped = sem("st_exped")
        max0_step = sem("max0_step")
        max1_step = sem("max1_step")
        max0_turned = sem("max0_turned")
        max1_turned = sem("max1_turned")
        max0_landed = sem("max0_landed")
        max1_landed = sem("max1_landed")
        t_read = sem("t_read")
        pv0_done = sem("pv0_done")
        pv1_done = sem("pv1_done")
        u0_copied = sem("u0_copied")
        u1_copied = sem("u1_copied")
        ut0_turned = sem("ut0_turned")
        ut1_turned = sem("ut1_turned")
        ut_read = sem("ut_read")
        xh1_turned = sem("xh1_turned")
        ff_ready = sem("ff_ready")
        router_step = sem("router_step")
        e2_ready = sem("e2_ready")
        gated_turned = sem("gated_turned")
        lora_done = sem("lora_done")
        norm1_step = sem("norm1_step")
        back_turned = sem("back_turned")
        w_rounded = sem("w_rounded")
        wq_step = sem("wq_step")
        w_total = sem("w_total")
        rms_step = sem("rms_step")
        xr_ready = sem("xr_ready")
        xq_turned = sem("xq_turned")
        hid_ready = sem("hid_ready")
        gelu_done = sem("gelu_done")
        hr_ready = sem("hr_ready")
        hq_turned = sem("hq_turned")
        y_ready = sem("y_ready")
        stored = sem("stored")
        in_step = sem("in_step")
        out_step = sem("out_step")
        w_step = sem("w_step")
        STREAM_DONE = sum(active(u, o) for u in range(FIRST, LAST + 1) for o in T_ORDER)

        block = ctx.enter_context(nc.Block())

        def stream(b):
            return xs[:, b * D:(b + 1) * D] if isinstance(b, int) else xs[:, bass.ts(b, D)]

        def iterations(engine, body):
            for t in range(FIRST, LOOP[0]):
                body(t, t % 2)
            with engine.Fori(0, (LOOP[1] - LOOP[0]) // 2) as turn:
                body(turn * 2 + LOOP[0], LOOP[0] % 2)
                body(turn * 2 + (LOOP[0] + 1), (LOOP[0] + 1) % 2)
            for t in range(LOOP[1], LAST + 1):
                body(t, t % 2)

        def plain(engine):
            engine.sem_inc(waited, 1)

        def run_rows(parts):
            return bass.AP(parts.tensor, parts.offset, [[D, RUN], [DH * PARTS * D, H1], [1, D]])

        def single_rows(parts, part):
            return bass.AP(parts.tensor, parts.offset + part * D,
                           [[PARTS * D, DH], [DH * PARTS * D, H1], [1, D]])

        def load_stack(sp, stack, odd, parts, singles, landed):
            view = stack[:, odd, :].rearrange("r (h l) -> r h l", h=H1)
            sp.dma_start(view[0:RUN], run_rows(parts)).then_inc(landed, 16)
            for n, part in enumerate(singles):
                r = RUN + n * DH
                sp.dma_start(view[r:r + DH], single_rows(parts, part)).then_inc(landed, 16)

        @block.sync
        def _(sp):
            def load_kv(b):
                sp.wait_ge(k_split_step, b * 4)
                sp.wait_ge(v0_placed, b)
                sp.dma_start(kv_in[:, :, :], kv[b]).then_inc(kv_landed, 16)

            def load_v1(b):
                sp.wait_ge(v1_placed, b)
                sp.dma_start(v1_in[:, :], kv[b, :, 0, :]).then_inc(v1_landed, 16)

            def store_k(b):
                sp.wait_ge(k_split_step, b * 4 + 4)
                sp.dma_start(k_parts[b].rearrange("l p c -> p l c"),
                             k_split[:, :, :, :].rearrange("p l t c -> p l (t c)")).then_inc(k_parts_out, 16)

            def store_q0(t):
                b = t + PREP
                sp.wait_ge(t_read, ordinal(T_ORDER, T_Q0, t) + 1)
                sp.dma_start(q0_parts[b], q0_t[:, :, :].rearrange("p t c -> p (t c)")).then_inc(q0_parts_out, 16)

            def store_q1(b):
                sp.wait_ge(ln2_step, b * 8 + 8)
                sp.dma_start(q1_parts[b], q1_split[:, :, :].rearrange("p t c -> p (t c)")).then_inc(q1_parts_out, 16)

            def load_stacks0(b, odd):
                if not (isinstance(b, int) and b < 2):
                    sp.wait_ge(pv0_done, b - 1)
                sp.wait_ge(k_parts_out, b * 16 + 16)
                load_stack(sp, k0, odd, k_parts[b, 0], [PARTS - 1 - n for n in K_SINGLE], k0_landed)
                sp.wait_ge(q0_parts_out, b * 16 + 16)
                load_stack(sp, q0, odd, q0_parts[b], Q_SINGLE, q0_landed)

            def load_k1(b, odd):
                if not (isinstance(b, int) and b < 2):
                    sp.wait_ge(pv1_done, b - 1)
                load_stack(sp, k1, odd, k_parts[b, 1], [PARTS - 1 - n for n in K_SINGLE], k1_landed)

            def load_q1(b, odd):
                sp.wait_ge(q1_parts_out, b * 16 + 16)
                load_stack(sp, q1, odd, q1_parts[b], Q_SINGLE, q1_landed)

            def max0_rows(t, odd):
                sp.wait_ge(t_read, ordinal(T_ORDER, T_MAX0, t) + 1)
                for n in range(2):
                    sp.dma_start(q0[STK + n:STK + n + 1, odd, :].rearrange("r (c q) -> r c q", c=H0),
                                 max0_t[n * H0:(n + 1) * H0, :]).then_inc(max0_landed, 16)

            def max1_rows(t, odd):
                sp.wait_ge(t_read, ordinal(T_ORDER, T_MAX1, t) + 1)
                for n in range(2):
                    sp.dma_start(q1[STK + n:STK + n + 1, odd, :].rearrange("r (h q) -> r h q", h=H1),
                                 max1_t[n * H1:(n + 1) * H1, :, :].rearrange("h f q -> h (f q)")).then_inc(max1_landed, 16)

            load_kv(0)
            for (first, end), landed in zip(X_GROUPS, x_landed):
                sp.dma_start(xs[:, first * D:end * D].rearrange("p (b d) -> p b d", d=D),
                             x[first:end].rearrange("b p d -> p b d")).then_inc(landed, 16)
            for dst, src in ((wff_sb[:, :, :], w_ff.rearrange("(k p) n -> p k n", p=P)),
                             (lora_b_sb[:, :], lora_b),
                             (base_b_all[:, :], base_b.partition_broadcast(P)),
                             (router_b_all[:, :], router_b.partition_broadcast(P)),
                             (attn_gamma_all[:, :], attn_gamma.partition_broadcast(P)),
                             (mlp_gamma_all[:, :], mlp_gamma.partition_broadcast(P))):
                sp.dma_start(dst, src).then_inc(weights_in, 16)

            def body(t, odd):
                if active(t, LATE):
                    max1_rows(t, (odd + LATE) % 2)
                if active(t, SCORE1):
                    store_q1(t + SCORE1)
                    load_k1(t + SCORE1, (odd + SCORE1) % 2)
                    load_q1(t + SCORE1, (odd + SCORE1) % 2)
                if active(t, SCORE0):
                    max0_rows(t, (odd + SCORE0) % 2)
                if active(t, SCORE1):
                    load_v1(t + SCORE1)
                if active(t, PREP):
                    store_k(t + PREP)
                if active(t, LOAD):
                    load_kv(t + LOAD)
                if active(t, PREP):
                    store_q0(t)
                    load_stacks0(t + PREP, (odd + PREP) % 2)
                if isinstance(t, int) and t == FIRST:
                    sp.dma_start(w1_sb[:, :].rearrange("p (k n) -> p k n", k=FT),
                                 w1.rearrange("(k p) n -> p k n", p=P)).then_inc(mlp_weights_in, 16)
                    sp.dma_start(w2_sb[:, :].rearrange("p (k n) -> p k n", k=HT),
                                 w2.rearrange("(k p) n -> p k n", p=P)).then_inc(mlp_weights_in, 16)

            iterations(sp, body)
            with sp.Fori(0, NB) as b:
                sp.wait_ge(out_step, b * 8 + 8)
                sp.dma_start(out[b], y[:, :]).then_inc(stored, 16)
            sp.wait_ge(stored, NB * 16)

        @block.gpsimd
        def _(pool):
            for tile, value in ((ident, 0.0), (ident_bf, 0.0), (mask_q, 0.0), (mask_k, 0.0)):
                pool.memset(tile[:], value).then_inc(masks_zeroed, 1)
            pool.iota(iota8_i[:, :], pattern=[[1, NE]], base=0, channel_multiplier=0).then_inc(masks_zeroed, 1)
            pool.wait_ge(masks_zeroed, 5)
            step = Steps(pool, consts_ready, 0, 11)
            step.done(pool.tensor_copy(iota8[:, :], iota8_i[:, :]))
            step.done(pool.memset(neg_half[:, :], -0.5))
            step.done(pool.memset(ones[:, :], 1.0))
            step.done(pool.memset(v0[:, :, :, :], 1.0))
            step.done(pool.memset(v1[:, :, :], 1.0))
            step.wait()
            step.done(pool.memset(k0[STK:STM, :, :], 1.0))
            step.done(pool.memset(k1[STK:STM, :, :], 1.0))
            step.wait()
            for m in (ident, ident_bf):
                step.done(pool.affine_select(out=m[:, :], in_=m[:, :], compare_op=ALU.not_equal, fill=1.0, base=0,
                                   pattern=[[-1, P]], channel_multiplier=1))
            step.done(pool.affine_select(out=mask_q[:, :, :], in_=mask_q[:, :, :], compare_op=ALU.is_ge, fill=MASKED, base=0,
                               pattern=[[0, G], [-1, P]], channel_multiplier=1))
            step.done(pool.affine_select(out=mask_k[:, :, :], in_=mask_k[:, :, :], compare_op=ALU.is_ge, fill=MASKED, base=0,
                               pattern=[[0, G], [1, P]], channel_multiplier=-1))
            pool.wait_ge(consts_ready, 11)

            def split_k_high(b):
                pool.wait_ge(kv_landed, b * 16 + 16)
                pool.wait_ge(k_parts_out, b * 16)
                step = Steps(pool, k_split_step, b, 4)
                plain(pool)
                step.done(pool.tensor_scalar(k_split[:, :, 2, :], kv_in[:, :, :], 1.0, None, ALU.mult)).wait()
                step.done(pool.tensor_tensor(k_rest[:, :, :], kv_in[:, :, :], k_split[:, :, 2, :], ALU.subtract))

            def split_k_mid(b):
                step = Steps(pool, k_split_step, b, 4)
                step.at = step.at + 2
                step.wait()
                plain(pool)
                step.done(pool.tensor_scalar(k_split[:, :, 1, :], k_rest[:, :, :], 1.0, None, ALU.mult))

            def split_k_low(b):
                step = Steps(pool, k_split_step, b, 4)
                step.at = step.at + 3
                step.wait()
                step.done(pool.tensor_tensor(k_split[:, :, 0, :], k_rest[:, :, :], k_split[:, :, 1, :], ALU.subtract))

            def place_v0(b, odd):
                pool.wait_ge(kv_landed, b * 16 + 16)
                if not (isinstance(b, int) and b < 2):
                    pool.wait_ge(pv0_done, b - 1)
                plain(pool)
                pool.tensor_scalar(v0[:, odd, :, 0:DH], kv_in[:, 1, :].rearrange("p (h d) -> p h d", d=DH), 1.0, None,
                                   ALU.mult).then_inc(v0_placed, 1)

            def place_v1(b):
                pool.wait_ge(v1_landed, b * 16 + 16)
                pool.wait_ge(pv1_done, b)
                plain(pool)
                pool.tensor_scalar(v1[:, :, 0:DH], v1_in[:, :].rearrange("p (h d) -> p h d", d=DH), 1.0, None,
                                   ALU.mult).then_inc(v1_placed, 1)

            def rstd(b, per, ln_step, after, mv, var, out_, sem_, steps):
                pool.wait_ge(ln_step, b * per + after)
                step = Steps(pool, sem_, b, steps)
                plain(pool)
                step.done(pool.tensor_scalar(var[:, :], mv[:, 1:2], LN_EPS, None, ALU.add)).wait()
                step.done(pool.tensor_tensor(out_[:, :], var[:, :], neg_half[:, :], ALU.pow))
                return step

            def mid(b):
                step = rstd(b, 5, ln1_step, 4, mv1, var1, rstd1, rstd1_step, 3)
                if isinstance(b, int) and b == 0:
                    pool.wait_ge(weights_in, 6 * 16)
                pool.wait_ge(ln2_step, b * 8)
                step.done(pool.tensor_tensor(x1b[:, :], x1[:, :], base_b_all[:, :], ALU.add))

            def body(t, odd):
                if active(t, PREP):
                    split_k_high(t + PREP)
                    rstd(t + PREP, 7, ln0_step, 2, mv0, var0, rstd0, rstd0_step, 2)
                    split_k_mid(t + PREP)
                if active(t, MID):
                    mid(t + MID)
                if active(t, PREP):
                    split_k_low(t + PREP)
                    place_v0(t + PREP, (odd + PREP) % 2)
                if active(t, MID):
                    rstd(t + MID, 8, ln2_step, 3, mv2, var2, rstd2, rstd2_step, 2)
                if active(t, SCORE1):
                    place_v1(t + SCORE1)

            iterations(pool, body)
            with pool.Fori(0, NB) as b:
                pool.wait_ge(in_step, b * 10 + 2)
                step = Steps(pool, rms_step, b, 2)
                plain(pool)
                step.done(pool.tensor_scalar(rms_in[:, :], mv3[:, 1:2], 1.0 + RMS_EPS, LN_EPS * RMS_EPS, ALU.mult,
                                             ALU.add)).wait()
                step.done(pool.tensor_tensor(rms[:, :], rms_in[:, :], neg_half[:, :], ALU.pow))

        @block.tensor
        def _(pe):
            pe.wait_ge(consts_ready, 11)

            def take_t(use, t):
                n = ordinal(T_ORDER, use, t)
                if not (isinstance(n, int) and n == 0):
                    pe.wait_ge(t_read, n)

            def take_ut(use, t):
                n = ordinal(UT_ORDER, use, t)
                if not (isinstance(n, int) and n == 0):
                    pe.wait_ge(ut_read, n)

            def take_s(use, t, order, freed):
                n = ordinal(order, use, t)
                if not (isinstance(n, int) and n < 2):
                    pe.wait_ge(freed, n - 1)

            def scores1(t, odd, h):
                b = t + SCORE1
                odd = (odd + SCORE1) % 2
                if h == 0:
                    pe.wait_ge(k1_landed, b * 64 + 64)
                    pe.wait_ge(q1_landed, b * 64 + 64)
                take_s(H0 // G + h, t, S_ORDER, s_reduced)
                for f in range(FT):
                    last = pe.matmul(ps_s[h % 2][:, f * D:(f + 1) * D], q1[0:STK, odd, h * D + f * P:h * D + (f + 1) * P],
                                     k1[0:STK, odd, h * D:(h + 1) * D], start=(f == 0), stop=True, skip_group_check=True)
                last.then_inc(s_ready, 1)

            def scores1_t(t, odd, h):
                b = t + LATE
                odd = (odd + LATE) % 2
                if h == 0:
                    pe.wait_ge(max1_landed, b * 32 + 32)
                take_s(H0 // G + h, t, ST_ORDER, st_exped)
                for f in range(FT):
                    last = pe.matmul(ps_st[h % 2][:, f * D:(f + 1) * D], k1[0:STM, odd, h * D + f * P:h * D + (f + 1) * P],
                                     q1[0:STM, odd, h * D:(h + 1) * D], start=(f == 0), stop=True, skip_group_check=True)
                last.then_inc(st_ready, 1)

            def scores0(t, odd, g):
                b = t + SCORE0
                odd = (odd + SCORE0) % 2
                if g == 0:
                    pe.wait_ge(k0_landed, b * 64 + 64)
                    pe.wait_ge(q0_landed, b * 64 + 64)
                take_s(g, t, S_ORDER, s_reduced)
                out_ = ps_s[g % 2]
                pe.matmul(out_[:, :], ident_bf[:, :], mask_q[:, :, :].rearrange("p g k -> p (g k)"), start=True,
                          stop=False, skip_group_check=True)
                for j in range(G):
                    c = (g * G + j) * P
                    last = pe.matmul(out_[:, j * P:(j + 1) * P], q0[0:STK, odd, c:c + P], k0[0:STK, odd, c:c + P], start=False,
                                     stop=(j == G - 1), skip_group_check=True)
                last.then_inc(s_ready, 1)

            def scores0_t(t, odd, g):
                b = t + MID
                if g == 0:
                    pe.wait_ge(max0_landed, b * 32 + 32)
                take_s(g, t, ST_ORDER, st_exped)
                out_ = ps_st[g % 2]
                pe.matmul(out_[:, :], ident_bf[:, :], mask_k[:, :, :].rearrange("p g k -> p (g k)"), start=True,
                          stop=False, skip_group_check=True)
                for j in range(G):
                    c = (g * G + j) * P
                    last = pe.matmul(out_[:, j * P:(j + 1) * P], k0[0:STM, odd, c:c + P], q0[0:STM, odd, c:c + P], start=False,
                                     stop=(j == G - 1), skip_group_check=True)
                last.then_inc(st_ready, 1)

            def pv0(t, odd, g):
                b = t + MID
                if g == 0:
                    pe.wait_ge(v0_placed, b + 1)
                    pe.wait_ge(u0_copied, b)
                    if not (isinstance(t, int) and t + LATE - 1 < 0):
                        pe.wait_ge(u1_copied, t + LATE)
                pe.wait_ge(st_exped, ordinal(ST_ORDER, g, t) + 1)
                for j in range(G):
                    h = column_head(g * G + j)
                    last = pe.matmul(ps_u[32 * j:32 * j + 32, g * P:(g + 1) * P],
                                     v0[:, odd, h, :],
                                     p0[:, g, j * P:(j + 1) * P], start=True, stop=True, skip_group_check=True)
                if g == H0 // G - 1:
                    last.then_inc(pv0_done, 1)

            def pv1(t, g):
                b = t + LATE
                if g == 0:
                    pe.wait_ge(v1_placed, b + 1)
                    pe.wait_ge(u0_copied, NB if isinstance(t, int) and t >= NB else t + MID + 1)
                    pe.wait_ge(u1_copied, b)
                pe.wait_ge(st_exped, ordinal(ST_ORDER, H0 // G + g * G + G - 1, t) + 1)
                for f in range(FT):
                    for j in range(G):
                        h = g * G + j
                        last = pe.matmul(ps_u[32 * j:32 * j + 32, g * D:(g + 1) * D],
                                         v1[:, f * H1 + h, :],
                                         p1[:, h, f * D:(f + 1) * D], start=(f == 0), stop=(f == FT - 1),
                                         skip_group_check=True)
                if g == H1 // G - 1:
                    last.then_inc(pv1_done, 1)

            def turn_u0(t):
                b = t + MID
                pe.wait_ge(u0_copied, b + 1)
                take_ut(0, t)
                for g in range(H0 // G):
                    last = pe.transpose(ps_ut[:, g * P:(g + 1) * P], u0[:, g, :], ident[:, :])
                last.then_inc(ut0_turned, 1)

            def turn_u1(t):
                b = t + LATE
                pe.wait_ge(u1_copied, b + 1)
                take_ut(1, t)
                for f in range(FT):
                    for g in range(H1 // G):
                        n = f * (H1 // G) + g
                        last = pe.transpose(ps_ut[:, n * P:(n + 1) * P], u1[:, g, f * P:(f + 1) * P], ident[:, :])
                last.then_inc(ut1_turned, 1)

            def turn_max1(t):
                b = t + LATE
                pe.wait_ge(max1_step, b * 2 + 2)
                take_t(T_MAX1, t)
                for f in range(FT):
                    last = pe.transpose(ps_t_h[0:2 * H1, f, :], max1_split[:, f, :, :].rearrange("p s h -> p (s h)"),
                                        ident_bf[:, :])
                last.then_inc(max1_turned, 1)

            def turn_max0(t):
                b = t + SCORE0
                pe.wait_ge(max0_step, b * 2 + 2)
                take_t(T_MAX0, t)
                pe.transpose(ps_t_h[0:2 * H0, 0, :], max0_split[:, :, :].rearrange("p s h -> p (s h)"),
                             ident_bf[:, :]).then_inc(max0_turned, 1)

            def moe(t):
                b = t + MID
                pe.wait_ge(ln1_step, b * 5 + 5)
                take_t(T_XH1, t)
                for f in range(FT):
                    last = pe.transpose(ps_t[:, f * P:(f + 1) * P], xh1[:, f * P:(f + 1) * P], ident[:, :])
                last.then_inc(xh1_turned, 1)
                pe.wait_ge(t_read, ordinal(T_ORDER, T_XH1, t) + 1)
                pe.wait_ge(ut_read, ordinal(UT_ORDER, 0, t) + 1)
                pe.wait_ge(ln2_step, b * 8)
                if isinstance(b, int) and b == 0:
                    pe.wait_ge(weights_in, 6 * 16)
                    pe.wait_ge(w_step, 3)
                for f in range(FT):
                    last = pe.matmul(ps_ut[:, 0:NFF - D], xh1_t[:, f, :], wff_sb[:, f, D:NFF], start=(f == 0),
                                     stop=(f == FT - 1), skip_group_check=True)
                last.then_inc(ff_ready, 1)
                for f in range(FT):
                    pe.matmul(ps_ff[:, 0:D], xh1_t[:, f, :], wff_sb[:, f, 0:D], start=(f == 0), stop=False,
                              skip_group_check=True)

            def turn_gated(t):
                b = t + MID
                pe.wait_ge(router_step, b * 12 + 12)
                take_t(T_GATED, t)
                pe.transpose(ps_t[:, 0:P], gated[:, :], ident[:, :]).then_inc(gated_turned, 1)

            def lora(t):
                pe.wait_ge(t_read, ordinal(T_ORDER, T_GATED, t) + 1)
                pe.matmul(ps_ff[:, 0:D], gated_t[:, :], lora_b_sb[:, :], start=False, stop=True,
                          skip_group_check=True).then_inc(lora_done, 1)

            def turn_q0(t):
                b = t + PREP
                pe.wait_ge(ln0_step, b * 7 + 7)
                take_t(T_Q0, t)
                for part in range(PARTS):
                    for f in range(FT):
                        last = pe.transpose(ps_t_h[:, part * FT + f, :], q0_split[:, part, f * P:(f + 1) * P],
                                            ident_bf[:, :])
                last.then_inc(q0_turned, 1)

            def turn_back(t):
                b = t + LATE
                pe.wait_ge(ut_read, ordinal(UT_ORDER, 1, t) + 1)
                take_t(T_BACK, t)
                for f in range(FT):
                    last = pe.transpose(ps_t[:, f * P:(f + 1) * P], a1[:, f, :], ident[:, :])
                last.then_inc(back_turned, 1)

            def body(t, odd):
                late, mid_, first, second = active(t, LATE), active(t, MID), active(t, SCORE0), active(t, SCORE1)
                if mid_:
                    scores0_t(t, odd, 0)
                    scores0_t(t, odd, 1)
                if first:
                    scores0(t, odd, 0)
                if mid_:
                    scores0_t(t, odd, 2)
                if late:
                    turn_max1(t)
                if first:
                    scores0(t, odd, 1)
                if mid_:
                    scores0_t(t, odd, 3)
                    for g in range(H0 // G):
                        pv0(t, odd, g)
                if first:
                    scores0(t, odd, 2)
                if mid_:
                    turn_u0(t)
                if first:
                    scores0(t, odd, 3)
                for h in range(G):
                    if late:
                        scores1_t(t, odd, h)
                if first:
                    turn_max0(t)
                if mid_:
                    moe(t)
                if late:
                    scores1_t(t, odd, G)
                if active(t, PREP):
                    turn_q0(t)
                for h in range(2):
                    if second:
                        scores1(t, odd, h)
                    if late:
                        scores1_t(t, odd, G + 1 + h)
                if late:
                    scores1_t(t, odd, H1 - 1)
                if mid_:
                    turn_gated(t)
                if late:
                    pv1(t, 0)
                if mid_:
                    lora(t)
                if second:
                    scores1(t, odd, 2)
                if late:
                    pv1(t, 1)
                if second:
                    scores1(t, odd, 3)
                    scores1(t, odd, 4)
                if late:
                    turn_u1(t)
                if second:
                    scores1(t, odd, 5)
                if late:
                    turn_back(t)
                if second:
                    scores1(t, odd, 6)
                    scores1(t, odd, 7)
                if isinstance(t, int) and t == FIRST + 1:
                    pe.wait_ge(w_step, 2)
                    pe.matmul(ps_ff[:, 0:2], ones[:, :], w_sum[:, :], start=True, stop=True).then_inc(w_total, 1)

            iterations(pe, body)

            def turn_input(b):
                pe.wait_ge(in_step, b * 10 + 9)
                for f in range(FT):
                    last = pe.transpose(ps_t_h[:, f, :], xq[:, f * P:(f + 1) * P], ident_bf[:, :])
                last.then_inc(xq_turned, 1)

            def up(b):
                pe.wait_ge(in_step, b * 10 + 10)
                pe.wait_ge(gelu_done, b * 2)
                for n in range(2):
                    for f in range(FT):
                        last = pe.matmul(ps_st[n][:, :], xq_t[:, f, :], w1_q[:, f, n * 512:(n + 1) * 512],
                                         start=(f == 0), stop=(f == FT - 1))
                    last.then_inc(hid_ready, 1)

            def turn_hidden(b):
                pe.wait_ge(out_step, b * 8 + 6)
                for k in range(HT):
                    last = pe.transpose(ps_ut_bf[:, k, :], hq[:, k * P:(k + 1) * P], ident_bf[:, :])
                last.then_inc(hq_turned, 1)

            def down(b):
                pe.wait_ge(out_step, b * 8 + 7)
                for k in range(HT):
                    last = pe.matmul(ps_ff[:, 0:D], hq_t[:, k, :], w2_q[:, k, :], start=(k == 0), stop=(k == HT - 1))
                last.then_inc(y_ready, 1)

            def mlp(b):
                turn_hidden(b)
                turn_input(b + 1)
                down(b)
                up(b + 1)

            pe.wait_ge(t_read, STREAM_DONE)
            pe.wait_ge(wq_step, 4)
            turn_input(0)
            up(0)
            with pe.Fori(0, NB - 1) as b:
                mlp(b)
            turn_hidden(NB - 1)
            down(NB - 1)

        @block.scalar
        def _(act):
            def exp0(t, g):
                b = t + MID
                if g == 0:
                    act.wait_ge(pv0_done, b)
                act.wait_ge(st_ready, ordinal(ST_ORDER, g, t) + 1)
                act.activation(p0[:, g, :], ps_st[g % 2][:, :], ACT.Exp, scale=SCALE).then_inc(st_exped, 1)

            def exp1(t, h):
                b = t + LATE
                if h == 0:
                    act.wait_ge(pv1_done, b)
                act.wait_ge(st_ready, ordinal(ST_ORDER, H0 // G + h, t) + 1)
                act.activation(p1[:, h, :], ps_st[h % 2][:, :], ACT.Exp, scale=SCALE).then_inc(st_exped, 1)

            def round_weight(n, w):
                act.wait_ge(w_step, 5)
                act.activation(w[:, :], w[:, :], ACT.Identity, scale=w_scale[:, n:n + 1],
                               bias=round_all[:, :]).then_inc(w_rounded, 1)

            def body(t, odd):
                late, mid_ = active(t, LATE), active(t, MID)
                b, bl = t + MID, t + LATE
                if mid_:
                    exp0(t, 0)
                    exp0(t, 1)
                    exp0(t, 2)
                if late:
                    act.wait_ge(max1_turned, bl + 1)
                    act.wait_ge(max1_landed, bl * 32)
                    act.copy(max1_t[:, :, :], ps_t_h[0:2 * H1, 0:FT, :]).then_inc(t_read, 1)
                if mid_:
                    exp0(t, 3)
                    act.wait_ge(pv0_done, b + 1)
                    act.wait_ge(ut0_turned, b)
                    act.copy(u0[:, :, :].rearrange("p g q -> p (g q)"), ps_u[:, :]).then_inc(u0_copied, 1)
                if late:
                    for h in range(G):
                        exp1(t, h)
                if active(t, SCORE0):
                    act.wait_ge(max0_turned, t + SCORE0 + 1)
                    act.wait_ge(max0_landed, (t + SCORE0) * 32)
                    act.copy(max0_t[:, :], ps_t_h[0:2 * H0, 0, :]).then_inc(t_read, 1)
                if mid_:
                    act.wait_ge(xh1_turned, b + 1)
                    act.copy(xh1_t[:, :, :].rearrange("p f q -> p (f q)"), ps_t[:, 0:D]).then_inc(t_read, 1)
                if late:
                    exp1(t, G)
                if mid_:
                    act.wait_ge(router_step, b * 12 + 3)
                    act.activation(e2[:, :], gap[:, :], ACT.Exp).then_inc(e2_ready, 1)
                if active(t, PREP):
                    act.wait_ge(q0_turned, t + PREP + 1)
                    act.wait_ge(q0_parts_out, (t + PREP) * 16)
                    act.copy(q0_t[:, :, :].rearrange("p t c -> p (t c)"), ps_t_bf[:, 0:PARTS * D]).then_inc(t_read, 1)
                if late:
                    exp1(t, G + 1)
                    exp1(t, G + 2)
                if mid_:
                    act.wait_ge(gated_turned, b + 1)
                    act.copy(gated_t[:, :], ps_t[:, 0:P]).then_inc(t_read, 1)
                if late:
                    exp1(t, G + 3)
                    act.wait_ge(pv1_done, bl + 1)
                    act.wait_ge(ut1_turned, bl)
                    act.copy(u1[:, :, :].rearrange("p g q -> p (g q)"), ps_u[:, :]).then_inc(u1_copied, 1)

                if isinstance(t, int) and t in W_ITERATIONS:
                    n = W_ITERATIONS.index(t)
                    round_weight(n, (w1_sb, w2_sb)[n])

            iterations(act, body)
            def round_input(b):
                act.wait_ge(in_step, b * 10 + 8)
                act.activation(xr[:, :], xn[:, :], ACT.Identity, scale=qscale[:, 0:1], bias=round_all[:, :]).then_inc(xr_ready, 1)

            def gelu(b):
                for n in range(2):
                    act.wait_ge(hid_ready, b * 2 + n + 1)
                    act.activation(hid[:, n * 512:(n + 1) * 512], ps_st[n][:, :], ACT.Gelu,
                                   scale=dequant[:, 0:1]).then_inc(gelu_done, 1)

            def round_hidden(b):
                act.wait_ge(out_step, b * 8 + 4)
                act.activation(hr[:, :], hid[:, :], ACT.Identity, scale=qscale[:, 1:2], bias=round_all[:, :]).then_inc(hr_ready, 1)

            def mlp(b):
                round_hidden(b)
                round_input(b + 1)
                gelu(b + 1)

            act.wait_ge(t_read, STREAM_DONE)
            round_input(0)
            gelu(0)
            with act.Fori(0, NB - 1) as b:
                mlp(b)
            round_hidden(NB - 1)

        @block.vector
        def _(dve):
            def row_stats(step, src, stats, mv):
                plain(dve)
                step.done(dve.bn_stats(stats[:, :], src)).wait()
                plain(dve)
                step.done(dve.bn_aggr(mv[:, :], stats[:, :]))

            def split_q(step, xh, rest, split):
                step.done(dve.tensor_copy(split[:, 0, :], xh[:, :])).wait()
                step.done(dve.tensor_tensor(rest[:, :], xh[:, :], split[:, 0, :], ALU.subtract)).wait()
                step.done(dve.tensor_copy(split[:, 1, :], rest[:, :])).wait()
                step.done(dve.tensor_tensor(split[:, 2, :], rest[:, :], split[:, 1, :], ALU.subtract))

            def normalise(out_, src, mv, rstd):
                return dve.tensor_scalar(out_[:, :], src, mv[:, 0:1], rstd[:, :], ALU.subtract, ALU.mult)

            def prep0_stats(b):
                group = next(i for i, (_, end) in enumerate(X_GROUPS) if b < end) if isinstance(b, int) else -1
                dve.wait_ge(x_landed[group], 16)
                row_stats(Steps(dve, ln0_step, b, 7), stream(b), stats0, mv0)

            def prep0(b):
                step = Steps(dve, ln0_step, b, 7)
                step.at = step.at + 2
                dve.wait_ge(rstd0_step, b * 2 + 2)
                dve.wait_ge(q0_turned, b)
                step.done(normalise(xh0, stream(b), mv0, rstd0)).wait()
                split_q(step, xh0, rest0, q0_split)

            def maxima(t, order, use, out_, src):
                dve.wait_ge(s_ready, ordinal(order, use, t) + 1)
                dve.tensor_reduce(out_, src, AX.X, ALU.max, negate=True).then_inc(s_reduced, 1)

            def split_max(step, top_, high, low):
                step.done(dve.tensor_copy(high, top_)).wait()
                step.done(dve.tensor_tensor(low, top_, high, ALU.subtract))

            def maxima0(t, g):
                maxima(t, S_ORDER, g, max0[:, g * G:(g + 1) * G], ps_s[g % 2][:, :].rearrange("p (j k) -> p j k", j=G))

            def maxima1(t, h):
                maxima(t, S_ORDER, H0 // G + h, max1[:, :, h], ps_s[h % 2][:, :].rearrange("p (f k) -> p f k", f=FT))

            def split_max0(t):
                b = t + SCORE0
                dve.wait_ge(s_reduced, ordinal(S_ORDER, H0 // G - 1, t) + 1)
                dve.wait_ge(max0_turned, b)
                split_max(Steps(dve, max0_step, b, 2), max0[:, :], max0_split[:, 0, :], max0_split[:, 1, :])

            def split_max1(t):
                b = t + SCORE1
                dve.wait_ge(s_reduced, ordinal(S_ORDER, H0 // G + H1 - 1, t) + 1)
                dve.wait_ge(max1_turned, b)
                split_max(Steps(dve, max1_step, b, 2), max1[:, :, :], max1_split[:, :, 0, :], max1_split[:, :, 1, :])

            def attention0_out(t):
                b = t + MID
                step = Steps(dve, ln1_step, b, 5)
                dve.wait_ge(ut0_turned, b + 1)
                ut = ps_ut[:, :].rearrange("p (c w) -> p c w", c=H0)
                step.done(dve.reciprocal(rz0[:, :], ut[:, :, DH])).wait()
                dve.tensor_tensor(a0[:, :].rearrange("p (f h d) -> p h f d", f=FT, d=DH),
                                  ps_ut[:, :].rearrange("p (h f w) -> p h f w", h=H1, f=FT)[:, :, :, 0:DH],
                                  rz0[:, :].rearrange("p (h f) -> p h f", f=FT).unsqueeze(3).broadcast_to([P, H1, FT, DH]),
                                  ALU.mult).then_inc(ut_read, 1)
                dve.wait_ge(ut_read, ordinal(UT_ORDER, 0, t) + 1)
                dve.wait_ge(rstd1_step, b * 3)
                step.done(dve.tensor_tensor(x1[:, :], a0[:, :], stream(b), ALU.add)).wait()
                row_stats(step, x1[:, :], stats1, mv1)

            def ln1(b):
                step = Steps(dve, ln1_step, b, 5)
                step.at = step.at + 4
                dve.wait_ge(rstd1_step, b * 3 + 2)
                dve.wait_ge(xh1_turned, b)
                step.done(normalise(xh1, x1[:, :], mv1, rstd1))

            def router(b):
                step = Steps(dve, router_step, b, 12)
                dve.wait_ge(ff_ready, b + 1)
                if isinstance(b, int) and b == 0:
                    dve.wait_ge(weights_in, 6 * 16)
                    dve.wait_ge(consts_ready, 11)
                step.done(dve.tensor_tensor(logits[:, :], ps_ut[:, ER:ER + NE], router_b_all[:, :], ALU.add)).wait()
                plain(dve)
                step.done(dve.max(top[:, :], logits[:, :])).wait()
                step.done(dve.tensor_tensor(gap[:, :], top[:, 1:2], top[:, 0:1], ALU.subtract))
                plain(dve)
                step.done(dve.max_index(top_i[:, :], top[:, :], logits[:, :]))

            def route(b):
                step = Steps(dve, router_step, b, 12)
                step.at = step.at + 4
                step.wait()
                step.done(dve.tensor_copy(top_if[:, :], top_i[:, 0:2]))
                dve.wait_ge(e2_ready, b + 1)
                step.done(dve.tensor_scalar(esum[:, :], e2[:, :], 1.0, 1.0 / LORA_SCALE, ALU.add, ALU.mult)).wait()
                step.done(dve.reciprocal(gate1[:, :], esum[:, :])).wait()
                step.done(dve.tensor_tensor(gate2[:, :], e2[:, :], gate1[:, :], ALU.mult)).wait()
                step.done(dve.tensor_scalar(pick1[:, :], iota8[:, :], top_if[:, 0:1], gate1[:, :], ALU.is_equal, ALU.mult))
                step.done(dve.tensor_scalar(pick2[:, :], iota8[:, :], top_if[:, 1:2], gate2[:, :], ALU.is_equal, ALU.mult)).wait()
                step.done(dve.tensor_tensor(gates[:, :], pick1[:, :], pick2[:, :], ALU.add)).wait()
                dve.wait_ge(gated_turned, b)
                step.done(dve.tensor_tensor(gated[:, :].rearrange("p (e r) -> p e r", e=NE),
                                            ps_ut[:, 0:ER].rearrange("p (e r) -> p e r", e=NE),
                                            gates[:, :].unsqueeze(2).broadcast_to([P, NE, ER // NE]), ALU.mult))

            def moe_out(b):
                step = Steps(dve, ln2_step, b, 8)
                dve.wait_ge(lora_done, b + 1)
                dve.wait_ge(rstd1_step, b * 3 + 3)
                here = stream(b)
                step.done(dve.tensor_tensor(here, ps_ff[:, 0:D], x1b[:, :], ALU.add)).wait()
                row_stats(step, here, stats2, mv2)

            def ln2(b):
                here = stream(b)
                step = Steps(dve, ln2_step, b, 8)
                step.at = step.at + 3
                dve.wait_ge(rstd2_step, b * 2 + 2)
                dve.wait_ge(q1_parts_out, b * 16)
                step.done(normalise(xh2, here, mv2, rstd2)).wait()
                split_q(step, xh2, rest2, q1_split)

            def attention1_out(t):
                b = t + LATE
                step = Steps(dve, norm1_step, b, 2)
                dve.wait_ge(ut1_turned, b + 1)
                ut = ps_ut[:, :].rearrange("p (c w) -> p c w", c=FT * H1)
                step.done(dve.reciprocal(rz1[:, :], ut[:, :, DH])).wait()
                step.done(dve.tensor_scalar(rzg1[:, :], rz1[:, :], attn_gamma_all[:, 0:1], None, ALU.mult)).wait()
                dve.tensor_tensor(a1[:, :, :].rearrange("p f (h d) -> p (f h) d", d=DH), ut[:, :, 0:DH],
                                  rzg1[:, :].unsqueeze(2).broadcast_to([P, FT * H1, DH]), ALU.mult).then_inc(ut_read, 1)

            def stream_out(t):
                b = t + LATE
                dve.wait_ge(back_turned, b + 1)
                here = stream(b)
                dve.tensor_tensor(here, ps_t[:, 0:D], here, ALU.add).then_inc(t_read, 1)

            def weight_scales():
                step = Steps(dve, w_step, 0, 5)
                dve.wait_ge(mlp_weights_in, 32)
                for n, w in enumerate((w1_sb, w2_sb)):
                    step.done(dve.tensor_reduce(w_sum[:, n:n + 1], w[:, :], AX.X, ALU.add, apply_absolute_value=True))
                dve.wait_ge(w_total, 1)
                step.done(dve.tensor_scalar(w_mean[:, :], ps_ff[:, 0:2], 1.0 / (D * HID), QEPS, ALU.mult, ALU.max)).wait()
                step.done(dve.reciprocal(w_scale[:, :], w_mean[:, :]))
                step.done(dve.memset(round_all[:, :], ROUND))

            def clip_weight(n, w_q, w):
                step = Steps(dve, wq_step, n, 2)
                flat = w_q[:, :, :].rearrange("p k n -> p (k n)")
                dve.wait_ge(w_rounded, n + 1)
                step.done(dve.tensor_scalar(flat, w[:, :], ROUND, 1.0, ALU.subtract, ALU.min)).wait()
                step.done(dve.tensor_scalar(flat, flat, -1.0, None, ALU.max))

            def body(t, odd):
                late, mid_, first, second = active(t, LATE), active(t, MID), active(t, SCORE0), active(t, SCORE1)
                if second:
                    ln2(t + SCORE1)
                if active(t, PREP):
                    prep0_stats(t + PREP)
                if first:
                    maxima0(t, 0)
                    maxima0(t, 1)
                    maxima0(t, 2)
                if mid_:
                    attention0_out(t)
                if first:
                    maxima0(t, 3)
                    split_max0(t)
                if mid_:
                    ln1(t + MID)
                if active(t, PREP):
                    prep0(t + PREP)
                if mid_:
                    router(t + MID)
                    route(t + MID)
                if second:
                    maxima1(t, 0)
                    maxima1(t, 1)
                if mid_:
                    moe_out(t + MID)
                if second:
                    maxima1(t, 2)
                    maxima1(t, 3)
                    maxima1(t, 4)
                if late:
                    attention1_out(t)
                if second:
                    maxima1(t, 5)
                    maxima1(t, 6)
                    maxima1(t, 7)
                    split_max1(t)
                if late:
                    stream_out(t)
                if isinstance(t, int) and t == FIRST + 1:
                    weight_scales()
                if isinstance(t, int) and t in W_ITERATIONS:
                    n = W_ITERATIONS.index(t)
                    clip_weight(n, (w1_q, w2_q)[n], (w1_sb, w2_sb)[n])

            iterations(dve, body)

            def quant_scales(step, n, src, row_scale, weight_scale):
                step.done(dve.tensor_reduce(amax[:, n:n + 1], src, AX.X, ALU.max, apply_absolute_value=True)).wait()
                if row_scale is None:
                    step.done(dve.tensor_scalar(amax_c[:, n:n + 1], amax[:, n:n + 1], QEPS, None, ALU.max)).wait()
                else:
                    step.done(dve.tensor_scalar(amax_c[:, n:n + 1], amax[:, n:n + 1], row_scale, QEPS, ALU.mult,
                                                ALU.max)).wait()
                step.done(dve.reciprocal(arec[:, n:n + 1], amax_c[:, n:n + 1])).wait()
                if row_scale is None:
                    step.done(dve.tensor_scalar(qscale[:, n:n + 1], arec[:, n:n + 1], 127.0, None, ALU.mult))
                else:
                    step.done(dve.tensor_scalar(qscale[:, n:n + 1], arec[:, n:n + 1], 127.0, row_scale, ALU.mult, ALU.mult))
                step.done(dve.tensor_scalar(dequant[:, n:n + 1], amax_c[:, n:n + 1], weight_scale, 1.0 / 127.0,
                                            ALU.mult, ALU.mult))

            def scale_input(b):
                step = Steps(dve, in_step, b, 10)
                row_stats(step, stream(b), stats3, mv3)
                step.wait()
                step.done(dve.scalar_tensor_tensor(out=xn[:, :], in0=stream(b), scalar=mv3[:, 0:1], in1=mlp_gamma_all[:, :],
                                                   op0=ALU.subtract, op1=ALU.mult)).wait()
                dve.wait_ge(gelu_done, b * 2)
                dve.wait_ge(rms_step, b * 2 + 2)
                quant_scales(step, 0, xn[:, :], rms[:, :], w_mean[:, 0:1])

            def quant_input(b):
                step = Steps(dve, in_step, b, 10)
                step.at = step.at + 8
                dve.wait_ge(xr_ready, b + 1)
                step.done(dve.tensor_scalar(xq[:, :], xr[:, :], ROUND, 127.0, ALU.subtract, ALU.min))

            def copy_input(b):
                step = Steps(dve, in_step, b, 10)
                step.at = step.at + 9
                dve.wait_ge(xq_turned, b + 1)
                step.done(dve.tensor_scalar(xq_t[:, :, :].rearrange("p f q -> p (f q)"), ps_t_bf[:, 0:D], -128.0, None, ALU.max))

            def scale_hidden(b):
                dve.wait_ge(gelu_done, b * 2 + 2)
                quant_scales(Steps(dve, out_step, b, 8), 1, hid[:, :], None, w_mean[:, 1:2])

            def quant_hidden(b):
                step = Steps(dve, out_step, b, 8)
                step.at = step.at + 5
                dve.wait_ge(hr_ready, b + 1)
                step.done(dve.tensor_scalar(hq[:, :], hr[:, :], ROUND, 127.0, ALU.subtract, ALU.min))

            def copy_hidden(b):
                step = Steps(dve, out_step, b, 8)
                step.at = step.at + 6
                dve.wait_ge(hq_turned, b + 1)
                step.done(dve.tensor_scalar(hq_t[:, :, :].rearrange("p k q -> p (k q)"),
                                            ps_ut_bf.rearrange("p k q -> p (k q)"), -128.0, None, ALU.max))

            def add_output(b):
                step = Steps(dve, out_step, b, 8)
                step.at = step.at + 7
                dve.wait_ge(y_ready, b + 1)
                dve.wait_ge(stored, b * 16)
                step.done(dve.scalar_tensor_tensor(out=y[:, :], in0=ps_ff[:, 0:D], scalar=dequant[:, 1:2], in1=stream(b),
                                                   op0=ALU.mult, op1=ALU.add))

            def mlp(b):
                scale_hidden(b)
                scale_input(b + 1)
                quant_hidden(b)
                quant_input(b + 1)
                copy_hidden(b)
                copy_input(b + 1)
                add_output(b)

            dve.wait_ge(t_read, STREAM_DONE)
            scale_input(0)
            quant_input(0)
            copy_input(0)
            with dve.Fori(0, NB - 1) as b:
                mlp(b)
            scale_hidden(NB - 1)
            quant_hidden(NB - 1)
            copy_hidden(NB - 1)
            add_output(NB - 1)


def kernel(**inputs):
    import numpy as np
    import concourse.bacc as bacc
    from concourse.bass_utils import run_bass_kernel_spmd

    a = {k: np.asarray(v) for k, v in inputs.items()}
    c = a["ctx_2048"]
    turned = c.reshape(NB, P, FT, P).transpose(0, 3, 2, 1).reshape(NB, P, D)
    lora_a = a["L0_ffn_lora_A"].transpose(1, 0, 2).reshape(D, ER)
    arrays = {
        "x": a["x"],
        "kv": np.stack([turned, c], axis=2),
        "w_ff": np.concatenate([a["L0_ffn_base_w"].T, lora_a, a["L0_ffn_router_w"].T], axis=1),
        "base_b": a["L0_ffn_base_b"],
        "router_b": a["L0_ffn_router_b"],
        "lora_b": a["L0_ffn_lora_B"].reshape(ER, D),
        "attn_gamma": a["L1_xattn_gamma"].reshape(1),
        "w1": a["L1_ffn_w1"].T,
        "w2": a["L1_ffn_w2"].T,
        "mlp_gamma": a["L1_ffn_gamma"],
    }
    nc = bacc.Bacc("TRN2", target_bir_lowering=False, num_devices=1)
    aps = {}
    for name, v in arrays.items():
        arrays[name] = v = np.ascontiguousarray(v)
        aps[name] = nc.dram_tensor(f"in_{name}", v.shape, mybir.dt.from_np(v.dtype), kind="ExternalInput").ap()
    out = nc.dram_tensor("out", (NB, P, D), F32, kind="ExternalOutput").ap()
    program(nc, out=out, **aps)
    r = run_bass_kernel_spmd(nc, [{f"in_{k}": v for k, v in arrays.items()}], core_ids=[0])
    return r.results[0]["out"]
```

```python
from contextlib import ExitStack

import concourse.bass as bass
from concourse import mybir

F32 = mybir.dt.float32
BF16 = mybir.dt.bfloat16
U32 = mybir.dt.uint32
I32 = mybir.dt.int32
ALU = mybir.AluOpType
ACT = mybir.ActivationFunctionType
AX = mybir.AxisListType

NB = 16
P = 128
D = 256
DH = 16
H0 = D // DH
H1 = P // DH
FT = D // P
NE = 8
ER = 128
NFF = D + ER + NE
HID = 1024
HT = HID // P
PARTS = 3
RUN = PARTS * DH
STK = 6 * DH
STM = STK + 2
G = 4
LN_EPS = 1e-5
RMS_EPS = 1e-6
QEPS = 1e-5
SCALE = DH ** -0.5
MASKED = -1e30
ROUND = 12582912.0
LORA_SCALE = 2.0

Q_SINGLE = (0, 0, 1)
K_SINGLE = (0, 1, 0)

LOAD, PREP, SCORE0, MID, SCORE1, LATE, BACK = 3, 2, 1, 0, -1, -2, -3
FIRST, LAST = -PREP, NB - 1 - BACK
W_ITERATIONS = (0, 1)
LOOP = (-BACK, NB - LOAD)

X_GROUPS = ((0, 1), (1, 2), (2, 4), (4, NB))

SCALE_IN, UP, HIDDEN, DOWN = 2, 1, 0, -1
MLP_FIRST, MLP_LAST = -SCALE_IN, NB - 1 - DOWN
MLP_LOOP = (1 - DOWN, NB - SCALE_IN)

S_ORDER = [SCORE0] * (H0 // G) + [SCORE1] * H1
ST_ORDER = [MID] * (H0 // G) + [LATE] * H1
T_MAX1, T_BACK, T_XH1, T_MAX0, T_GATED, T_Q0 = range(6)
T_ORDER = [LATE, BACK, MID, SCORE0, MID, PREP]
UT_ORDER = [MID, LATE]


def active(t, offset):
    return not isinstance(t, int) or 0 <= t + offset < NB


def ordinal(order, n, t):
    start = t if isinstance(t, int) else LOOP[0]
    before = sum(active(u, o) for u in range(FIRST, start) for o in order)
    here = sum(active(t, o) for o in order[:n])
    return before + here if isinstance(t, int) else (t - LOOP[0]) * len(order) + before + here


class Steps:

    def __init__(self, engine, sem, b, per):
        self.engine, self.sem, self.at = engine, sem, b * per

    def done(self, instruction):
        instruction.then_inc(self.sem, 1)
        self.at = self.at + 1
        return self

    def wait(self):
        self.engine.wait_ge(self.sem, self.at)


def head_column(h):
    return (h % H1) * FT + h // H1


def column_head(c):
    return (c % FT) * H1 + c // FT


def program(nc, x, kv, w_ff, base_b, router_b, lora_b, attn_gamma, w1, w2, mlp_gamma, out):
    with ExitStack() as ctx:
        def sb(name, shape, dt=F32):
            return ctx.enter_context(nc.sbuf_tensor(name, shape, dt))

        def bank(name, shape, dt=F32):
            return ctx.enter_context(nc.psum_tensor(name, shape, dt))

        def sem(name):
            return ctx.enter_context(nc.semaphore(name))

        k_parts = nc.dram_tensor("k_parts", [NB, 2, P, PARTS * D], BF16, kind="Internal").ap()
        q0_parts = nc.dram_tensor("q0_parts", [NB, P, PARTS * D], BF16, kind="Internal").ap()
        q1_parts = nc.dram_tensor("q1_parts", [NB, P, PARTS * D], BF16, kind="Internal").ap()

        ident = sb("ident", [P, P])
        ident_bf = sb("ident_bf", [P, P], BF16)
        mask_q = sb("mask_q", [P, G, P], BF16)
        mask_k = sb("mask_k", [P, G, P], BF16)
        iota8 = sb("iota8", [P, NE])
        iota8_i = sb("iota8_i", [P, NE], I32)
        neg_half = sb("neg_half", [P, 1])
        ones = sb("ones", [P, P])
        wff_sb = sb("wff_sb", [P, FT, NFF])
        lora_b_sb = sb("lora_b_sb", [ER, D])
        base_b_all = sb("base_b_all", [P, D])
        router_b_all = sb("router_b_all", [P, NE])
        attn_gamma_all = sb("attn_gamma_all", [P, 1])
        mlp_gamma_all = sb("mlp_gamma_all", [P, D])
        w1_sb = sb("w1_sb", [P, FT * HID])
        w2_sb = sb("w2_sb", [P, HT * D])
        w1_q = sb("w1_q", [P, FT, HID], BF16)
        w2_q = sb("w2_q", [P, HT, D], BF16)
        w_sum = sb("w_sum", [P, 2])
        w_mean = sb("w_mean", [P, 2])
        w_scale = sb("w_scale", [P, 2])
        round_all = sb("round_all", [P, 1])

        kv_in = sb("kv_in", [P, 2, D])
        v1_in = sb("v1_in", [P, D])
        k_split = sb("k_split", [P, 2, PARTS, D], BF16)
        k_rest = sb("k_rest", [P, 2, D])
        k0 = sb("k0", [STM, 2, H0 * P], BF16)
        k1 = sb("k1", [STM, 2, H1 * D], BF16)
        q0 = sb("q0", [STM, 2, H0 * P], BF16)
        q1 = sb("q1", [STM, 2, H1 * D], BF16)
        v0 = sb("v0", [P, 2, H0, 2 * DH])
        v1 = sb("v1", [P, FT * H1, 2 * DH])
        xs = sb("xs", [P, NB * D])
        stats0 = sb("stats0", [P, 6])
        stats1 = sb("stats1", [P, 6])
        stats2 = sb("stats2", [P, 6])
        mv0 = sb("mv0", [P, 2])
        mv1 = sb("mv1", [P, 2])
        mv2 = sb("mv2", [P, 2])
        var0 = sb("var0", [P, 1])
        var1 = sb("var1", [P, 1])
        var2 = sb("var2", [P, 1])
        rstd0 = sb("rstd0", [P, 1])
        rstd1 = sb("rstd1", [P, 1])
        rstd2 = sb("rstd2", [P, 1])
        xh0 = sb("xh0", [P, D])
        rest0 = sb("rest0", [P, D])
        q0_split = sb("q0_split", [P, PARTS, D], BF16)
        q0_t = sb("q0_t", [P, PARTS, D], BF16)
        xh2 = sb("xh2", [P, D])
        rest2 = sb("rest2", [P, D])
        q1_split = sb("q1_split", [P, PARTS, D], BF16)
        max0 = sb("max0", [P, H0])
        max0_split = sb("max0_split", [P, 2, H0], BF16)
        max0_t = sb("max0_t", [2 * H0, P], BF16)
        max1 = sb("max1", [P, FT, H1])
        max1_split = sb("max1_split", [P, FT, 2, H1], BF16)
        max1_t = sb("max1_t", [2 * H1, FT, P], BF16)
        p0 = sb("p0", [P, H0 // G, G * P])
        p1 = sb("p1", [P, H1, FT * D])
        u0 = sb("u0", [P, H0 // G, P])
        u1 = sb("u1", [P, H1 // G, D])
        rz0 = sb("rz0", [P, H0])
        rz1 = sb("rz1", [P, FT * H1])
        rzg1 = sb("rzg1", [P, FT * H1])
        a0 = sb("a0", [P, D])
        a1 = sb("a1", [P, FT, P])
        x1 = sb("x1", [P, D])
        x1b = sb("x1b", [P, D])
        xh1 = sb("xh1", [P, D])
        xh1_t = sb("xh1_t", [P, FT, P])
        logits = sb("logits", [P, NE])
        top = sb("top", [P, NE])
        top_i = sb("top_i", [P, NE], U32)
        top_if = sb("top_if", [P, 2])
        gap = sb("gap", [P, 1])
        e2 = sb("e2", [P, 1])
        esum = sb("esum", [P, 1])
        gate1 = sb("gate1", [P, 1])
        gate1s = sb("gate1s", [P, 1])
        gate2 = sb("gate2", [P, 1])
        pick1 = sb("pick1", [P, NE])
        pick2 = sb("pick2", [P, NE])
        gates = sb("gates", [P, NE])
        gated = sb("gated", [P, ER])
        gated_t = sb("gated_t", [ER, P])

        stats3 = sb("stats3", [P, 6])
        mv3 = sb("mv3", [P, 2])
        rms_in = sb("rms_in", [P, 1])
        rms = sb("rms", [P, 1])
        xn = sb("xn", [P, D])
        amax = sb("amax", [P, 2])
        amax_c = sb("amax_c", [P, 2])
        arec = sb("arec", [P, 2])
        qscale = sb("qscale", [P, 2])
        dequant = sb("dequant", [P, 2])
        xr = sb("xr", [P, D])
        xq = sb("xq", [P, D], BF16)
        xq_t = sb("xq_t", [P, FT, P], BF16)
        hid = sb("hid", [P, HID])
        hr = sb("hr", [P, HID])
        hq = sb("hq", [P, HID], BF16)
        hq_t = sb("hq_t", [P, HT, P], BF16)
        y = sb("y", [P, D])

        ps_s = [bank(f"ps_s{i}", [P, G * P]) for i in range(2)]
        ps_st = [bank(f"ps_st{i}", [P, G * P]) for i in range(2)]
        ps_u = bank("ps_u", [P, 512])
        ps_t = bank("ps_t", [P, 512])
        ps_ff = bank("ps_ff", [P, 512])
        ps_ut = bank("ps_ut", [P, 512])
        ps_t_bf = ps_t[:, :].bitcast(BF16)
        ps_t_h = ps_t_bf.rearrange("p (n q) -> p n q", q=P)
        ps_ut_bf = ps_ut[:, :].bitcast(BF16).rearrange("p (n q) -> p n q", q=P)

        consts_ready = sem("consts_ready")
        ones_ready = sem("ones_ready")
        masks_zeroed = sem("masks_zeroed")
        waited = sem("waited")
        weights_in = sem("weights_in")
        mlp_weights_in = sem("mlp_weights_in")
        kv_landed = sem("kv_landed")
        k_split_step = sem("k_split_step")
        k_parts_out = sem("k_parts_out")
        k0_landed = sem("k0_landed")
        k1_landed = sem("k1_landed")
        x_landed = [sem(f"x_landed{i}") for i in range(len(X_GROUPS))]
        v1_landed = sem("v1_landed")
        v0_placed = sem("v0_placed")
        v1_placed = sem("v1_placed")
        ln0_step = sem("ln0_step")
        q0_split_step = sem("q0_split_step")
        ln1_step = sem("ln1_step")
        ln2_step = sem("ln2_step")
        rstd0_step = sem("rstd0_step")
        rstd1_step = sem("rstd1_step")
        rstd2_step = sem("rstd2_step")
        q0_turned = sem("q0_turned")
        q0_parts_out = sem("q0_parts_out")
        q0_landed = sem("q0_landed")
        q1_parts_out = sem("q1_parts_out")
        q1_landed = sem("q1_landed")
        s_ready = sem("s_ready")
        s_reduced = sem("s_reduced")
        st_ready = sem("st_ready")
        st_exped = sem("st_exped")
        max0_step = sem("max0_step")
        max1_step = sem("max1_step")
        max0_turned = sem("max0_turned")
        max1_turned = sem("max1_turned")
        max0_landed = sem("max0_landed")
        max1_landed = sem("max1_landed")
        t_read = sem("t_read")
        pv0_done = sem("pv0_done")
        pv1_done = sem("pv1_done")
        u0_copied = sem("u0_copied")
        u1_copied = sem("u1_copied")
        ut0_turned = sem("ut0_turned")
        ut1_turned = sem("ut1_turned")
        ut_read = sem("ut_read")
        xh1_turned = sem("xh1_turned")
        ff_ready = sem("ff_ready")
        router_step = sem("router_step")
        e2_ready = sem("e2_ready")
        gated_turned = sem("gated_turned")
        lora_done = sem("lora_done")
        norm1_step = sem("norm1_step")
        back_turned = sem("back_turned")
        w_rounded = sem("w_rounded")
        wq_step = sem("wq_step")
        w_total = sem("w_total")
        rms_step = sem("rms_step")
        xr_ready = sem("xr_ready")
        xq_turned = sem("xq_turned")
        hid_ready = sem("hid_ready")
        gelu_done = sem("gelu_done")
        hr_ready = sem("hr_ready")
        hq_turned = sem("hq_turned")
        y_ready = sem("y_ready")
        stored = sem("stored")
        in_step = sem("in_step")
        xq_step = sem("xq_step")
        hid_step = sem("hid_step")
        hq_ready = sem("hq_ready")
        down_step = sem("down_step")
        w_step = sem("w_step")
        STREAM_DONE = sum(active(u, o) for u in range(FIRST, LAST + 1) for o in T_ORDER)

        block = ctx.enter_context(nc.Block())

        def stream(b):
            return xs[:, b * D:(b + 1) * D] if isinstance(b, int) else xs[:, bass.ts(b, D)]

        def iterations(engine, body):
            for t in range(FIRST, LOOP[0]):
                body(t, t % 2)
            with engine.Fori(0, (LOOP[1] - LOOP[0]) // 2) as turn:
                body(turn * 2 + LOOP[0], LOOP[0] % 2)
                body(turn * 2 + (LOOP[0] + 1), (LOOP[0] + 1) % 2)
            for t in range(LOOP[1], LAST + 1):
                body(t, t % 2)

        def mlp_iterations(engine, body):
            for t in range(MLP_FIRST, MLP_LOOP[0]):
                body(t)
            with engine.Fori(*MLP_LOOP) as t:
                body(t)
            for t in range(MLP_LOOP[1], MLP_LAST + 1):
                body(t)

        def plain(engine):
            engine.sem_inc(waited, 1)

        def run_rows(parts):
            return bass.AP(parts.tensor, parts.offset, [[D, RUN], [DH * PARTS * D, H1], [1, D]])

        def single_rows(parts, part):
            return bass.AP(parts.tensor, parts.offset + part * D,
                           [[PARTS * D, DH], [DH * PARTS * D, H1], [1, D]])

        def load_stack(sp, stack, odd, parts, singles, landed):
            view = stack[:, odd, :].rearrange("r (h l) -> r h l", h=H1)
            sp.dma_start(view[0:RUN], run_rows(parts)).then_inc(landed, 16)
            for n, part in enumerate(singles):
                r = RUN + n * DH
                sp.dma_start(view[r:r + DH], single_rows(parts, part)).then_inc(landed, 16)

        @block.sync
        def _(sp):
            def load_kv(b):
                sp.wait_ge(k_split_step, b * 4)
                sp.wait_ge(v0_placed, b)
                sp.dma_start(kv_in[:, :, :], kv[b]).then_inc(kv_landed, 16)

            def load_v1(b):
                sp.wait_ge(v1_placed, b)
                sp.dma_start(v1_in[:, :], kv[b, :, 0, :]).then_inc(v1_landed, 16)

            def store_k(b):
                sp.wait_ge(k_split_step, b * 4 + 4)
                sp.dma_start(k_parts[b].rearrange("l p c -> p l c"),
                             k_split[:, :, :, :].rearrange("p l t c -> p l (t c)")).then_inc(k_parts_out, 16)

            def store_q0(t):
                b = t + PREP
                sp.wait_ge(t_read, ordinal(T_ORDER, T_Q0, t) + 1)
                sp.dma_start(q0_parts[b], q0_t[:, :, :].rearrange("p t c -> p (t c)")).then_inc(q0_parts_out, 16)

            def store_q1(b):
                sp.wait_ge(ln2_step, b * 8 + 8)
                sp.dma_start(q1_parts[b], q1_split[:, :, :].rearrange("p t c -> p (t c)")).then_inc(q1_parts_out, 16)

            def load_k0(b, odd):
                if not (isinstance(b, int) and b < 2):
                    sp.wait_ge(pv0_done, b - 1)
                sp.wait_ge(k_parts_out, b * 16 + 16)
                load_stack(sp, k0, odd, k_parts[b, 0], [PARTS - 1 - n for n in K_SINGLE], k0_landed)

            def load_q0(b, odd):
                sp.wait_ge(q0_parts_out, b * 16 + 16)
                load_stack(sp, q0, odd, q0_parts[b], Q_SINGLE, q0_landed)

            def load_k1(b, odd):
                if not (isinstance(b, int) and b < 2):
                    sp.wait_ge(pv1_done, b - 1)
                load_stack(sp, k1, odd, k_parts[b, 1], [PARTS - 1 - n for n in K_SINGLE], k1_landed)

            def load_q1(b, odd):
                sp.wait_ge(q1_parts_out, b * 16 + 16)
                load_stack(sp, q1, odd, q1_parts[b], Q_SINGLE, q1_landed)

            def max0_rows(t, odd):
                sp.wait_ge(t_read, ordinal(T_ORDER, T_MAX0, t) + 1)
                for n in range(2):
                    sp.dma_start(q0[STK + n:STK + n + 1, odd, :].rearrange("r (c q) -> r c q", c=H0),
                                 max0_t[n * H0:(n + 1) * H0, :]).then_inc(max0_landed, 16)

            def max1_rows(t, odd):
                sp.wait_ge(t_read, ordinal(T_ORDER, T_MAX1, t) + 1)
                for n in range(2):
                    sp.dma_start(q1[STK + n:STK + n + 1, odd, :].rearrange("r (h q) -> r h q", h=H1),
                                 max1_t[n * H1:(n + 1) * H1, :, :].rearrange("h f q -> h (f q)")).then_inc(max1_landed, 16)

            load_kv(0)
            for (first, end), landed in zip(X_GROUPS, x_landed):
                sp.dma_start(xs[:, first * D:end * D].rearrange("p (b d) -> p b d", d=D),
                             x[first:end].rearrange("b p d -> p b d")).then_inc(landed, 16)
            for dst, src in ((wff_sb[:, :, :], w_ff.rearrange("(k p) n -> p k n", p=P)),
                             (lora_b_sb[:, :], lora_b),
                             (base_b_all[:, :], base_b.partition_broadcast(P)),
                             (router_b_all[:, :], router_b.partition_broadcast(P)),
                             (attn_gamma_all[:, :], attn_gamma.partition_broadcast(P)),
                             (mlp_gamma_all[:, :], mlp_gamma.partition_broadcast(P))):
                sp.dma_start(dst, src).then_inc(weights_in, 16)

            def body(t, odd):
                if active(t, LATE):
                    max1_rows(t, (odd + LATE) % 2)
                if active(t, SCORE1):
                    store_q1(t + SCORE1)
                    load_k1(t + SCORE1, (odd + SCORE1) % 2)
                    load_q1(t + SCORE1, (odd + SCORE1) % 2)
                if active(t, SCORE1):
                    load_v1(t + SCORE1)
                if active(t, PREP):
                    store_k(t + PREP)
                if active(t, SCORE0):
                    max0_rows(t, (odd + SCORE0) % 2)
                if active(t, PREP):
                    load_k0(t + PREP, (odd + PREP) % 2)
                if active(t, LOAD):
                    load_kv(t + LOAD)
                if active(t, PREP):
                    store_q0(t)
                    load_q0(t + PREP, (odd + PREP) % 2)
                if isinstance(t, int) and t == FIRST:
                    sp.dma_start(w1_sb[:, :].rearrange("p (k n) -> p k n", k=FT),
                                 w1.rearrange("(k p) n -> p k n", p=P)).then_inc(mlp_weights_in, 16)
                    sp.dma_start(w2_sb[:, :].rearrange("p (k n) -> p k n", k=HT),
                                 w2.rearrange("(k p) n -> p k n", p=P)).then_inc(mlp_weights_in, 16)

            iterations(sp, body)
            with sp.Fori(0, NB) as b:
                sp.wait_ge(down_step, b * 2 + 2)
                sp.dma_start(out[b], y[:, :]).then_inc(stored, 16)
            sp.wait_ge(stored, NB * 16)

        @block.gpsimd
        def _(pool):
            for tile, value in ((ident, 0.0), (ident_bf, 0.0), (mask_q, 0.0), (mask_k, 0.0)):
                pool.memset(tile[:], value).then_inc(masks_zeroed, 1)
            pool.iota(iota8_i[:, :], pattern=[[1, NE]], base=0, channel_multiplier=0).then_inc(masks_zeroed, 1)
            pool.wait_ge(masks_zeroed, 5)
            step = Steps(pool, consts_ready, 0, 7)
            step.done(pool.tensor_copy(iota8[:, :], iota8_i[:, :]))
            step.done(pool.memset(neg_half[:, :], -0.5))
            step.done(pool.memset(ones[:, :], 1.0))
            for m in (ident, ident_bf):
                step.done(pool.affine_select(out=m[:, :], in_=m[:, :], compare_op=ALU.not_equal, fill=1.0, base=0,
                                   pattern=[[-1, P]], channel_multiplier=1))
            step.done(pool.affine_select(out=mask_q[:, :, :], in_=mask_q[:, :, :], compare_op=ALU.is_ge, fill=MASKED, base=0,
                               pattern=[[0, G], [-1, P]], channel_multiplier=1))
            step.done(pool.affine_select(out=mask_k[:, :, :], in_=mask_k[:, :, :], compare_op=ALU.is_ge, fill=MASKED, base=0,
                               pattern=[[0, G], [1, P]], channel_multiplier=-1))
            pool.wait_ge(consts_ready, 7)

            def split_k_high(b):
                pool.wait_ge(kv_landed, b * 16 + 16)
                pool.wait_ge(k_parts_out, b * 16)
                step = Steps(pool, k_split_step, b, 4)
                plain(pool)
                step.done(pool.tensor_scalar(k_split[:, :, 2, :], kv_in[:, :, :], 1.0, None, ALU.mult)).wait()
                step.done(pool.tensor_tensor(k_rest[:, :, :], kv_in[:, :, :], k_split[:, :, 2, :], ALU.subtract))

            def split_k_mid(b):
                step = Steps(pool, k_split_step, b, 4)
                step.at = step.at + 2
                step.wait()
                plain(pool)
                step.done(pool.tensor_scalar(k_split[:, :, 1, :], k_rest[:, :, :], 1.0, None, ALU.mult))

            def split_k_low(b):
                step = Steps(pool, k_split_step, b, 4)
                step.at = step.at + 3
                step.wait()
                step.done(pool.tensor_tensor(k_split[:, :, 0, :], k_rest[:, :, :], k_split[:, :, 1, :], ALU.subtract))

            def split_q0(b):
                pool.wait_ge(ln0_step, b * 3 + 3)
                pool.wait_ge(q0_turned, b)
                step = Steps(pool, q0_split_step, b, 4)
                plain(pool)
                step.done(pool.tensor_scalar(q0_split[:, 0, :], xh0[:, :], 1.0, None, ALU.mult)).wait()
                step.done(pool.tensor_tensor(rest0[:, :], xh0[:, :], q0_split[:, 0, :], ALU.subtract)).wait()
                plain(pool)
                step.done(pool.tensor_scalar(q0_split[:, 1, :], rest0[:, :], 1.0, None, ALU.mult)).wait()
                step.done(pool.tensor_tensor(q0_split[:, 2, :], rest0[:, :], q0_split[:, 1, :], ALU.subtract))

            def place_v0(b, odd):
                if isinstance(b, int) and b == 0:
                    pool.wait_ge(ones_ready, 3)
                pool.wait_ge(kv_landed, b * 16 + 16)
                if not (isinstance(b, int) and b < 2):
                    pool.wait_ge(pv0_done, b - 1)
                plain(pool)
                pool.tensor_scalar(v0[:, odd, :, 0:DH], kv_in[:, 1, :].rearrange("p (h d) -> p h d", d=DH), 1.0, None,
                                   ALU.mult).then_inc(v0_placed, 1)

            def place_v1(b):
                pool.wait_ge(v1_landed, b * 16 + 16)
                pool.wait_ge(pv1_done, b)
                plain(pool)
                pool.tensor_scalar(v1[:, :, 0:DH], v1_in[:, :].rearrange("p (h d) -> p h d", d=DH), 1.0, None,
                                   ALU.mult).then_inc(v1_placed, 1)

            def rstd(b, per, ln_step, after, mv, var, out_, sem_, steps):
                pool.wait_ge(ln_step, b * per + after)
                step = Steps(pool, sem_, b, steps)
                plain(pool)
                step.done(pool.tensor_scalar(var[:, :], mv[:, 1:2], LN_EPS, None, ALU.add)).wait()
                step.done(pool.tensor_tensor(out_[:, :], var[:, :], neg_half[:, :], ALU.pow))
                return step

            def mid(b):
                step = rstd(b, 5, ln1_step, 4, mv1, var1, rstd1, rstd1_step, 3)
                if isinstance(b, int) and b == 0:
                    pool.wait_ge(weights_in, 6 * 16)
                pool.wait_ge(ln2_step, b * 8)
                step.done(pool.tensor_tensor(x1b[:, :], x1[:, :], base_b_all[:, :], ALU.add))

            def body(t, odd):
                if active(t, PREP):
                    split_k_high(t + PREP)
                    rstd(t + PREP, 3, ln0_step, 2, mv0, var0, rstd0, rstd0_step, 2)
                    split_k_mid(t + PREP)
                if active(t, MID):
                    mid(t + MID)
                if active(t, PREP):
                    split_k_low(t + PREP)
                    split_q0(t + PREP)
                    place_v0(t + PREP, (odd + PREP) % 2)
                if active(t, MID):
                    rstd(t + MID, 8, ln2_step, 3, mv2, var2, rstd2, rstd2_step, 2)
                if active(t, SCORE1):
                    place_v1(t + SCORE1)

            iterations(pool, body)
            with pool.Fori(0, NB) as b:
                pool.wait_ge(in_step, b * 8 + 2)
                step = Steps(pool, rms_step, b, 2)
                plain(pool)
                step.done(pool.tensor_scalar(rms_in[:, :], mv3[:, 1:2], 1.0 + RMS_EPS, LN_EPS * RMS_EPS, ALU.mult,
                                             ALU.add)).wait()
                step.done(pool.tensor_tensor(rms[:, :], rms_in[:, :], neg_half[:, :], ALU.pow))

        @block.tensor
        def _(pe):
            pe.wait_ge(consts_ready, 7)
            pe.wait_ge(ones_ready, 3)

            def take_t(use, t):
                n = ordinal(T_ORDER, use, t)
                if not (isinstance(n, int) and n == 0):
                    pe.wait_ge(t_read, n)

            def take_ut(use, t):
                n = ordinal(UT_ORDER, use, t)
                if not (isinstance(n, int) and n == 0):
                    pe.wait_ge(ut_read, n)

            def take_s(use, t, order, freed):
                n = ordinal(order, use, t)
                if not (isinstance(n, int) and n < 2):
                    pe.wait_ge(freed, n - 1)

            def scores1(t, odd, h):
                b = t + SCORE1
                odd = (odd + SCORE1) % 2
                if h == 0:
                    pe.wait_ge(k1_landed, b * 64 + 64)
                    pe.wait_ge(q1_landed, b * 64 + 64)
                take_s(H0 // G + h, t, S_ORDER, s_reduced)
                for f in range(FT):
                    last = pe.matmul(ps_s[h % 2][:, f * D:(f + 1) * D], q1[0:STK, odd, h * D + f * P:h * D + (f + 1) * P],
                                     k1[0:STK, odd, h * D:(h + 1) * D], start=(f == 0), stop=True, skip_group_check=True)
                last.then_inc(s_ready, 1)

            def scores1_t(t, odd, h):
                b = t + LATE
                odd = (odd + LATE) % 2
                if isinstance(b, int) and b == 0:
                    pe.wait_ge(ones_ready, 4)
                if h == 0:
                    pe.wait_ge(max1_landed, b * 32 + 32)
                take_s(H0 // G + h, t, ST_ORDER, st_exped)
                for f in range(FT):
                    last = pe.matmul(ps_st[h % 2][:, f * D:(f + 1) * D], k1[0:STM, odd, h * D + f * P:h * D + (f + 1) * P],
                                     q1[0:STM, odd, h * D:(h + 1) * D], start=(f == 0), stop=True, skip_group_check=True)
                last.then_inc(st_ready, 1)

            def scores0(t, odd, g):
                b = t + SCORE0
                odd = (odd + SCORE0) % 2
                if g == 0:
                    pe.wait_ge(k0_landed, b * 64 + 64)
                    pe.wait_ge(q0_landed, b * 64 + 64)
                take_s(g, t, S_ORDER, s_reduced)
                out_ = ps_s[g % 2]
                pe.matmul(out_[:, :], ident_bf[:, :], mask_q[:, :, :].rearrange("p g k -> p (g k)"), start=True,
                          stop=False, skip_group_check=True)
                for j in range(G):
                    c = (g * G + j) * P
                    last = pe.matmul(out_[:, j * P:(j + 1) * P], q0[0:STK, odd, c:c + P], k0[0:STK, odd, c:c + P], start=False,
                                     stop=(j == G - 1), skip_group_check=True)
                last.then_inc(s_ready, 1)

            def scores0_t(t, odd, g):
                b = t + MID
                if g == 0:
                    pe.wait_ge(max0_landed, b * 32 + 32)
                take_s(g, t, ST_ORDER, st_exped)
                out_ = ps_st[g % 2]
                pe.matmul(out_[:, :], ident_bf[:, :], mask_k[:, :, :].rearrange("p g k -> p (g k)"), start=True,
                          stop=False, skip_group_check=True)
                for j in range(G):
                    c = (g * G + j) * P
                    last = pe.matmul(out_[:, j * P:(j + 1) * P], k0[0:STM, odd, c:c + P], q0[0:STM, odd, c:c + P], start=False,
                                     stop=(j == G - 1), skip_group_check=True)
                last.then_inc(st_ready, 1)

            def pv0(t, odd, g):
                b = t + MID
                if g == 0:
                    pe.wait_ge(v0_placed, b + 1)
                    pe.wait_ge(u0_copied, b)
                    if not (isinstance(t, int) and t + LATE - 1 < 0):
                        pe.wait_ge(u1_copied, t + LATE)
                pe.wait_ge(st_exped, ordinal(ST_ORDER, g, t) + 1)
                for j in range(G):
                    h = column_head(g * G + j)
                    last = pe.matmul(ps_u[32 * j:32 * j + 32, g * P:(g + 1) * P],
                                     v0[:, odd, h, :],
                                     p0[:, g, j * P:(j + 1) * P], start=True, stop=True, skip_group_check=True)
                if g == H0 // G - 1:
                    last.then_inc(pv0_done, 1)

            def pv1(t, g, f):
                b = t + LATE
                if g == 0 and f == 0:
                    pe.wait_ge(v1_placed, b + 1)
                    pe.wait_ge(u0_copied, NB if isinstance(t, int) and t >= NB else t + MID + 1)
                    pe.wait_ge(u1_copied, b)
                pe.wait_ge(st_exped, ordinal(ST_ORDER, H0 // G + g * G + G - 1, t) + 1)
                for j in range(G):
                    h = g * G + j
                    last = pe.matmul(ps_u[32 * j:32 * j + 32, g * D:(g + 1) * D], v1[:, f * H1 + h, :],
                                     p1[:, h, f * D:(f + 1) * D], start=(f == 0), stop=(f == FT - 1),
                                     skip_group_check=True)
                if g == H1 // G - 1 and f == FT - 1:
                    last.then_inc(pv1_done, 1)

            def turn_u0(t):
                b = t + MID
                pe.wait_ge(u0_copied, b + 1)
                take_ut(0, t)
                for g in range(H0 // G):
                    last = pe.transpose(ps_ut[:, g * P:(g + 1) * P], u0[:, g, :], ident[:, :])
                last.then_inc(ut0_turned, 1)

            def turn_u1(t):
                b = t + LATE
                pe.wait_ge(u1_copied, b + 1)
                take_ut(1, t)
                for f in range(FT):
                    for g in range(H1 // G):
                        n = f * (H1 // G) + g
                        last = pe.transpose(ps_ut[:, n * P:(n + 1) * P], u1[:, g, f * P:(f + 1) * P], ident[:, :])
                last.then_inc(ut1_turned, 1)

            def turn_max1(t):
                b = t + LATE
                pe.wait_ge(max1_step, b * 2 + 2)
                take_t(T_MAX1, t)
                for f in range(FT):
                    last = pe.transpose(ps_t_h[0:2 * H1, f, :], max1_split[:, f, :, :].rearrange("p s h -> p (s h)"),
                                        ident_bf[:, :])
                last.then_inc(max1_turned, 1)

            def turn_max0(t):
                b = t + SCORE0
                pe.wait_ge(max0_step, b * 2 + 2)
                take_t(T_MAX0, t)
                pe.transpose(ps_t_h[0:2 * H0, 0, :], max0_split[:, :, :].rearrange("p s h -> p (s h)"),
                             ident_bf[:, :]).then_inc(max0_turned, 1)

            def moe(t):
                b = t + MID
                pe.wait_ge(ln1_step, b * 5 + 5)
                take_t(T_XH1, t)
                for f in range(FT):
                    last = pe.transpose(ps_t[:, f * P:(f + 1) * P], xh1[:, f * P:(f + 1) * P], ident[:, :])
                last.then_inc(xh1_turned, 1)
                pe.wait_ge(t_read, ordinal(T_ORDER, T_XH1, t) + 1)
                pe.wait_ge(ut_read, ordinal(UT_ORDER, 0, t) + 1)
                pe.wait_ge(ln2_step, b * 8)
                if isinstance(b, int) and b == 0:
                    pe.wait_ge(weights_in, 6 * 16)
                    pe.wait_ge(w_step, 3)
                for f in range(FT):
                    last = pe.matmul(ps_ut[:, 0:NFF - D], xh1_t[:, f, :], wff_sb[:, f, D:NFF], start=(f == 0),
                                     stop=(f == FT - 1), skip_group_check=True)
                last.then_inc(ff_ready, 1)
                for f in range(FT):
                    pe.matmul(ps_ff[:, 0:D], xh1_t[:, f, :], wff_sb[:, f, 0:D], start=(f == 0), stop=False,
                              skip_group_check=True)

            def turn_gated(t):
                b = t + MID
                pe.wait_ge(router_step, b * 12 + 12)
                take_t(T_GATED, t)
                pe.transpose(ps_t[:, 0:P], gated[:, :], ident[:, :]).then_inc(gated_turned, 1)

            def lora(t):
                pe.wait_ge(t_read, ordinal(T_ORDER, T_GATED, t) + 1)
                pe.matmul(ps_ff[:, 0:D], gated_t[:, :], lora_b_sb[:, :], start=False, stop=True,
                          skip_group_check=True).then_inc(lora_done, 1)

            def turn_q0(t):
                b = t + PREP
                pe.wait_ge(q0_split_step, b * 4 + 4)
                take_t(T_Q0, t)
                for part in range(PARTS):
                    for f in range(FT):
                        last = pe.transpose(ps_t_h[:, part * FT + f, :], q0_split[:, part, f * P:(f + 1) * P],
                                            ident_bf[:, :])
                last.then_inc(q0_turned, 1)

            def turn_back(t):
                pe.wait_ge(ut_read, ordinal(UT_ORDER, 0, t))
                take_t(T_BACK, t)
                for f in range(FT):
                    last = pe.transpose(ps_t[:, f * P:(f + 1) * P], a1[:, f, :], ident[:, :])
                last.then_inc(back_turned, 1)

            def body(t, odd):
                late, mid_, first, second = active(t, LATE), active(t, MID), active(t, SCORE0), active(t, SCORE1)
                if mid_:
                    for g in range(H0 // G):
                        scores0_t(t, odd, g)
                if late:
                    turn_max1(t)
                if mid_:
                    for g in range(H0 // G):
                        pv0(t, odd, g)
                if active(t, BACK):
                    turn_back(t)
                if first:
                    scores0(t, odd, 0)
                if mid_:
                    turn_u0(t)
                if first:
                    scores0(t, odd, 1)
                if late:
                    scores1_t(t, odd, 0)
                if first:
                    scores0(t, odd, 2)
                if late:
                    for h in range(1, G):
                        scores1_t(t, odd, h)
                if first:
                    scores0(t, odd, 3)
                if mid_:
                    moe(t)
                if first:
                    turn_max0(t)
                if late:
                    scores1_t(t, odd, G)
                if second:
                    scores1(t, odd, 0)
                if mid_:
                    turn_gated(t)
                if late:
                    scores1_t(t, odd, G + 1)
                if second:
                    scores1(t, odd, 1)
                if late:
                    scores1_t(t, odd, G + 2)
                if mid_:
                    lora(t)
                if second:
                    scores1(t, odd, 2)
                if active(t, PREP):
                    turn_q0(t)
                if late:
                    scores1_t(t, odd, G + 3)
                    pv1(t, 0, 0)
                if late:
                    pv1(t, 0, 1)
                if second:
                    scores1(t, odd, 3)
                if late:
                    pv1(t, 1, 0)
                if second:
                    scores1(t, odd, 4)
                if late:
                    pv1(t, 1, 1)
                if second:
                    scores1(t, odd, 5)
                    scores1(t, odd, 6)
                if late:
                    turn_u1(t)
                if second:
                    scores1(t, odd, 7)
                if isinstance(t, int) and t == FIRST + 1:
                    pe.wait_ge(w_step, 2)
                    pe.matmul(ps_ff[:, 0:2], ones[:, :], w_sum[:, :], start=True, stop=True).then_inc(w_total, 1)

            iterations(pe, body)

            def turn_input(b):
                pe.wait_ge(xq_step, b * 2 + 1)
                for f in range(FT):
                    last = pe.transpose(ps_t_h[:, f, :], xq[:, f * P:(f + 1) * P], ident_bf[:, :])
                last.then_inc(xq_turned, 1)

            def up(b):
                pe.wait_ge(xq_step, b * 2 + 2)
                pe.wait_ge(gelu_done, b * 2)
                for n in range(2):
                    for f in range(FT):
                        last = pe.matmul(ps_st[n][:, :], xq_t[:, f, :], w1_q[:, f, n * 512:(n + 1) * 512],
                                         start=(f == 0), stop=(f == FT - 1))
                    last.then_inc(hid_ready, 1)

            def turn_hidden(b):
                pe.wait_ge(hq_ready, b + 1)
                for k in range(HT):
                    last = pe.transpose(ps_ut_bf[:, k, :], hq[:, k * P:(k + 1) * P], ident_bf[:, :])
                last.then_inc(hq_turned, 1)

            def down(b):
                pe.wait_ge(down_step, b * 2 + 1)
                for k in range(HT):
                    last = pe.matmul(ps_ff[:, 0:D], hq_t[:, k, :], w2_q[:, k, :], start=(k == 0), stop=(k == HT - 1))
                last.then_inc(y_ready, 1)

            def mlp(t):
                if active(t, UP):
                    turn_input(t + UP)
                if active(t, UP):
                    up(t + UP)
                if active(t, DOWN):
                    down(t + DOWN)
                if active(t, HIDDEN):
                    turn_hidden(t + HIDDEN)

            pe.wait_ge(t_read, STREAM_DONE)
            pe.wait_ge(wq_step, 4)
            mlp_iterations(pe, mlp)

        @block.scalar
        def _(act):
            def exp0(t, g):
                b = t + MID
                if g == 0:
                    act.wait_ge(pv0_done, b)
                act.wait_ge(st_ready, ordinal(ST_ORDER, g, t) + 1)
                act.activation(p0[:, g, :], ps_st[g % 2][:, :], ACT.Exp, scale=SCALE).then_inc(st_exped, 1)

            def exp1(t, h):
                b = t + LATE
                if h == 0:
                    act.wait_ge(pv1_done, b)
                act.wait_ge(st_ready, ordinal(ST_ORDER, H0 // G + h, t) + 1)
                act.activation(p1[:, h, :], ps_st[h % 2][:, :], ACT.Exp, scale=SCALE).then_inc(st_exped, 1)

            def round_weight(n, w):
                act.wait_ge(w_step, 5)
                act.activation(w[:, :], w[:, :], ACT.Identity, scale=w_scale[:, n:n + 1],
                               bias=round_all[:, :]).then_inc(w_rounded, 1)

            def body(t, odd):
                late, mid_ = active(t, LATE), active(t, MID)
                b, bl = t + MID, t + LATE
                if mid_:
                    for g in range(H0 // G):
                        exp0(t, g)
                if late:
                    act.wait_ge(max1_turned, bl + 1)
                    act.wait_ge(max1_landed, bl * 32)
                    act.copy(max1_t[:, :, :], ps_t_h[0:2 * H1, 0:FT, :]).then_inc(t_read, 1)
                if mid_:
                    act.wait_ge(pv0_done, b + 1)
                    act.wait_ge(ut0_turned, b)
                    act.copy(u0[:, :, :].rearrange("p g q -> p (g q)"), ps_u[:, :]).then_inc(u0_copied, 1)
                if late:
                    for h in range(G):
                        exp1(t, h)
                if mid_:
                    act.wait_ge(xh1_turned, b + 1)
                    act.copy(xh1_t[:, :, :].rearrange("p f q -> p (f q)"), ps_t[:, 0:D]).then_inc(t_read, 1)
                    act.wait_ge(router_step, b * 12 + 3)
                    act.activation(e2[:, :], gap[:, :], ACT.Exp).then_inc(e2_ready, 1)
                if active(t, SCORE0):
                    act.wait_ge(max0_turned, t + SCORE0 + 1)
                    act.wait_ge(max0_landed, (t + SCORE0) * 32)
                    act.copy(max0_t[:, :], ps_t_h[0:2 * H0, 0, :]).then_inc(t_read, 1)
                if late:
                    exp1(t, G)
                if mid_:
                    act.wait_ge(gated_turned, b + 1)
                    act.copy(gated_t[:, :], ps_t[:, 0:P]).then_inc(t_read, 1)
                if late:
                    exp1(t, G + 1)
                    exp1(t, G + 2)
                if active(t, PREP):
                    act.wait_ge(q0_turned, t + PREP + 1)
                    act.wait_ge(q0_parts_out, (t + PREP) * 16)
                    act.copy(q0_t[:, :, :].rearrange("p t c -> p (t c)"), ps_t_bf[:, 0:PARTS * D]).then_inc(t_read, 1)
                if late:
                    exp1(t, G + 3)
                    act.wait_ge(pv1_done, bl + 1)
                    act.wait_ge(ut1_turned, bl)
                    act.copy(u1[:, :, :].rearrange("p g q -> p (g q)"), ps_u[:, :]).then_inc(u1_copied, 1)
                if isinstance(t, int) and t in W_ITERATIONS:
                    n = W_ITERATIONS.index(t)
                    round_weight(n, (w1_sb, w2_sb)[n])

            iterations(act, body)
            def round_input(b):
                act.wait_ge(in_step, b * 8 + 7)
                act.activation(xr[:, :], xn[:, :], ACT.Identity, scale=qscale[:, 0:1], bias=round_all[:, :]).then_inc(xr_ready, 1)

            def gelu(b):
                act.wait_ge(hr_ready, b)
                act.wait_ge(in_step, b * 8 + 8)
                for n in range(2):
                    act.wait_ge(hid_ready, b * 2 + n + 1)
                    act.activation(hid[:, n * 512:(n + 1) * 512], ps_st[n][:, :], ACT.Gelu,
                                   scale=dequant[:, 0:1]).then_inc(gelu_done, 1)

            def round_hidden(b):
                act.wait_ge(hid_step, b * 5 + 4)
                act.activation(hr[:, :], hid[:, :], ACT.Identity, scale=qscale[:, 1:2], bias=round_all[:, :]).then_inc(hr_ready, 1)

            def mlp(t):
                if active(t, HIDDEN):
                    round_hidden(t + HIDDEN)
                if active(t, UP):
                    gelu(t + UP)
                if active(t, SCALE_IN):
                    round_input(t + SCALE_IN)

            act.wait_ge(t_read, STREAM_DONE)
            mlp_iterations(act, mlp)

        @block.vector
        def _(dve):
            for tile in (v0[:, :, :, :], v1[:, :, :], k0[STK:STM, :, :]):
                dve.memset(tile, 1.0).then_inc(ones_ready, 1)

            def row_stats(step, src, stats, mv):
                plain(dve)
                step.done(dve.bn_stats(stats[:, :], src)).wait()
                plain(dve)
                step.done(dve.bn_aggr(mv[:, :], stats[:, :]))

            def split_q(step, xh, rest, split):
                step.done(dve.tensor_copy(split[:, 0, :], xh[:, :])).wait()
                step.done(dve.tensor_tensor(rest[:, :], xh[:, :], split[:, 0, :], ALU.subtract)).wait()
                step.done(dve.tensor_copy(split[:, 1, :], rest[:, :])).wait()
                step.done(dve.tensor_tensor(split[:, 2, :], rest[:, :], split[:, 1, :], ALU.subtract))

            def normalise(out_, src, mv, rstd):
                return dve.tensor_scalar(out_[:, :], src, mv[:, 0:1], rstd[:, :], ALU.subtract, ALU.mult)

            def prep0_stats(b):
                group = next(i for i, (_, end) in enumerate(X_GROUPS) if b < end) if isinstance(b, int) else -1
                dve.wait_ge(x_landed[group], 16)
                row_stats(Steps(dve, ln0_step, b, 3), stream(b), stats0, mv0)

            def prep0(b):
                step = Steps(dve, ln0_step, b, 3)
                step.at = step.at + 2
                dve.wait_ge(rstd0_step, b * 2 + 2)
                dve.wait_ge(q0_split_step, b * 4)
                step.done(normalise(xh0, stream(b), mv0, rstd0))

            def maxima(t, order, use, out_, src):
                dve.wait_ge(s_ready, ordinal(order, use, t) + 1)
                dve.tensor_reduce(out_, src, AX.X, ALU.max, negate=True).then_inc(s_reduced, 1)

            def split_max(step, top_, high, low):
                step.done(dve.tensor_copy(high, top_)).wait()
                step.done(dve.tensor_tensor(low, top_, high, ALU.subtract))

            def maxima0(t, g):
                maxima(t, S_ORDER, g, max0[:, g * G:(g + 1) * G], ps_s[g % 2][:, :].rearrange("p (j k) -> p j k", j=G))

            def maxima1(t, h):
                maxima(t, S_ORDER, H0 // G + h, max1[:, :, h], ps_s[h % 2][:, :].rearrange("p (f k) -> p f k", f=FT))

            def split_max0(t):
                b = t + SCORE0
                dve.wait_ge(s_reduced, ordinal(S_ORDER, H0 // G - 1, t) + 1)
                dve.wait_ge(max0_turned, b)
                split_max(Steps(dve, max0_step, b, 2), max0[:, :], max0_split[:, 0, :], max0_split[:, 1, :])

            def split_max1(t):
                b = t + SCORE1
                dve.wait_ge(s_reduced, ordinal(S_ORDER, H0 // G + H1 - 1, t) + 1)
                dve.wait_ge(max1_turned, b)
                split_max(Steps(dve, max1_step, b, 2), max1[:, :, :], max1_split[:, :, 0, :], max1_split[:, :, 1, :])

            def attention0_out(t):
                b = t + MID
                step = Steps(dve, ln1_step, b, 5)
                dve.wait_ge(ut0_turned, b + 1)
                ut = ps_ut[:, :].rearrange("p (c w) -> p c w", c=H0)
                step.done(dve.reciprocal(rz0[:, :], ut[:, :, DH])).wait()
                dve.tensor_tensor(a0[:, :].rearrange("p (f h d) -> p h f d", f=FT, d=DH),
                                  ps_ut[:, :].rearrange("p (h f w) -> p h f w", h=H1, f=FT)[:, :, :, 0:DH],
                                  rz0[:, :].rearrange("p (h f) -> p h f", f=FT).unsqueeze(3).broadcast_to([P, H1, FT, DH]),
                                  ALU.mult).then_inc(ut_read, 1)
                dve.wait_ge(ut_read, ordinal(UT_ORDER, 0, t) + 1)
                dve.wait_ge(rstd1_step, b * 3)
                step.done(dve.tensor_tensor(x1[:, :], a0[:, :], stream(b), ALU.add)).wait()
                row_stats(step, x1[:, :], stats1, mv1)

            def ln1(b):
                step = Steps(dve, ln1_step, b, 5)
                step.at = step.at + 4
                dve.wait_ge(rstd1_step, b * 3 + 2)
                dve.wait_ge(xh1_turned, b)
                step.done(normalise(xh1, x1[:, :], mv1, rstd1))

            def router(b):
                step = Steps(dve, router_step, b, 12)
                dve.wait_ge(ff_ready, b + 1)
                if isinstance(b, int) and b == 0:
                    dve.wait_ge(weights_in, 6 * 16)
                    dve.wait_ge(consts_ready, 7)
                step.done(dve.tensor_tensor(logits[:, :], ps_ut[:, ER:ER + NE], router_b_all[:, :], ALU.add)).wait()
                plain(dve)
                step.done(dve.max(top[:, :], logits[:, :])).wait()
                step.done(dve.tensor_tensor(gap[:, :], top[:, 1:2], top[:, 0:1], ALU.subtract))
                plain(dve)
                step.done(dve.max_index(top_i[:, :], top[:, :], logits[:, :]))

            def route(b):
                step = Steps(dve, router_step, b, 12)
                step.at = step.at + 4
                step.wait()
                step.done(dve.tensor_copy(top_if[:, :], top_i[:, 0:2]))
                dve.wait_ge(e2_ready, b + 1)
                step.done(dve.tensor_scalar(esum[:, :], e2[:, :], 1.0, 1.0 / LORA_SCALE, ALU.add, ALU.mult)).wait()
                step.done(dve.reciprocal(gate1[:, :], esum[:, :])).wait()
                step.done(dve.tensor_tensor(gate2[:, :], e2[:, :], gate1[:, :], ALU.mult)).wait()
                step.done(dve.tensor_scalar(pick1[:, :], iota8[:, :], top_if[:, 0:1], gate1[:, :], ALU.is_equal, ALU.mult))
                step.done(dve.tensor_scalar(pick2[:, :], iota8[:, :], top_if[:, 1:2], gate2[:, :], ALU.is_equal, ALU.mult)).wait()
                step.done(dve.tensor_tensor(gates[:, :], pick1[:, :], pick2[:, :], ALU.add)).wait()
                dve.wait_ge(gated_turned, b)
                step.done(dve.tensor_tensor(gated[:, :].rearrange("p (e r) -> p e r", e=NE),
                                            ps_ut[:, 0:ER].rearrange("p (e r) -> p e r", e=NE),
                                            gates[:, :].unsqueeze(2).broadcast_to([P, NE, ER // NE]), ALU.mult))

            def moe_out(b):
                step = Steps(dve, ln2_step, b, 8)
                dve.wait_ge(lora_done, b + 1)
                dve.wait_ge(rstd1_step, b * 3 + 3)
                here = stream(b)
                step.done(dve.tensor_tensor(here, ps_ff[:, 0:D], x1b[:, :], ALU.add)).wait()
                row_stats(step, here, stats2, mv2)

            def ln2(b):
                here = stream(b)
                step = Steps(dve, ln2_step, b, 8)
                step.at = step.at + 3
                dve.wait_ge(rstd2_step, b * 2 + 2)
                dve.wait_ge(q1_parts_out, b * 16)
                step.done(normalise(xh2, here, mv2, rstd2)).wait()
                split_q(step, xh2, rest2, q1_split)

            def attention1_out(t):
                b = t + LATE
                step = Steps(dve, norm1_step, b, 2)
                dve.wait_ge(ut1_turned, b + 1)
                ut = ps_ut[:, :].rearrange("p (c w) -> p c w", c=FT * H1)
                step.done(dve.reciprocal(rz1[:, :], ut[:, :, DH])).wait()
                step.done(dve.tensor_scalar(rzg1[:, :], rz1[:, :], attn_gamma_all[:, 0:1], None, ALU.mult)).wait()
                dve.tensor_tensor(a1[:, :, :].rearrange("p f (h d) -> p (f h) d", d=DH), ut[:, :, 0:DH],
                                  rzg1[:, :].unsqueeze(2).broadcast_to([P, FT * H1, DH]), ALU.mult).then_inc(ut_read, 1)

            def stream_out(t):
                b = t + BACK
                dve.wait_ge(back_turned, b + 1)
                here = stream(b)
                dve.tensor_tensor(here, ps_t[:, 0:D], here, ALU.add).then_inc(t_read, 1)

            def weight_scales():
                step = Steps(dve, w_step, 0, 5)
                dve.wait_ge(mlp_weights_in, 32)
                for n, w in enumerate((w1_sb, w2_sb)):
                    step.done(dve.tensor_reduce(w_sum[:, n:n + 1], w[:, :], AX.X, ALU.add, apply_absolute_value=True))
                dve.wait_ge(w_total, 1)
                step.done(dve.tensor_scalar(w_mean[:, :], ps_ff[:, 0:2], 1.0 / (D * HID), QEPS, ALU.mult, ALU.max)).wait()
                step.done(dve.reciprocal(w_scale[:, :], w_mean[:, :]))
                step.done(dve.memset(round_all[:, :], ROUND))

            def clip_weight(n, w_q, w):
                step = Steps(dve, wq_step, n, 2)
                flat = w_q[:, :, :].rearrange("p k n -> p (k n)")
                dve.wait_ge(w_rounded, n + 1)
                step.done(dve.tensor_scalar(flat, w[:, :], ROUND, 1.0, ALU.subtract, ALU.min)).wait()
                step.done(dve.tensor_scalar(flat, flat, -1.0, None, ALU.max))

            def body(t, odd):
                late, mid_, first, second = active(t, LATE), active(t, MID), active(t, SCORE0), active(t, SCORE1)
                if second:
                    ln2(t + SCORE1)
                if active(t, PREP):
                    prep0_stats(t + PREP)
                if first:
                    maxima0(t, 0)
                if active(t, BACK):
                    stream_out(t)
                if mid_:
                    attention0_out(t)
                if first:
                    maxima0(t, 1)
                if mid_:
                    ln1(t + MID)
                if active(t, PREP):
                    prep0(t + PREP)
                if first:
                    maxima0(t, 2)
                    maxima0(t, 3)
                    split_max0(t)
                if mid_:
                    router(t + MID)
                    route(t + MID)
                if second:
                    maxima1(t, 0)
                    maxima1(t, 1)
                if mid_:
                    moe_out(t + MID)
                if second:
                    for h in range(2, H1 - 1):
                        maxima1(t, h)
                if late:
                    attention1_out(t)
                if second:
                    maxima1(t, H1 - 1)
                    split_max1(t)
                if isinstance(t, int) and t == FIRST + 1:
                    weight_scales()
                if isinstance(t, int) and t in W_ITERATIONS:
                    n = W_ITERATIONS.index(t)
                    clip_weight(n, (w1_q, w2_q)[n], (w1_sb, w2_sb)[n])
                if isinstance(t, int) and t == FIRST:
                    dve.memset(k1[STK:STM, :, :], 1.0).then_inc(ones_ready, 1)

            iterations(dve, body)

            def scale_input_stats(b):
                row_stats(Steps(dve, in_step, b, 8), stream(b), stats3, mv3)

            def scale_input_max(b):
                step = Steps(dve, in_step, b, 8)
                step.at = step.at + 2
                step.wait()
                step.done(dve.scalar_tensor_tensor(out=xn[:, :], in0=stream(b), scalar=mv3[:, 0:1], in1=mlp_gamma_all[:, :],
                                                   op0=ALU.subtract, op1=ALU.mult)).wait()
                step.done(dve.tensor_reduce(amax[:, 0:1], xn[:, :], AX.X, ALU.max, apply_absolute_value=True))

            def scale_input(b):
                step = Steps(dve, in_step, b, 8)
                step.at = step.at + 4
                step.wait()
                dve.wait_ge(rms_step, b * 2 + 2)
                step.done(dve.tensor_scalar(amax_c[:, 0:1], amax[:, 0:1], rms[:, :], QEPS, ALU.mult, ALU.max)).wait()
                step.done(dve.reciprocal(arec[:, 0:1], amax_c[:, 0:1])).wait()
                step.done(dve.tensor_scalar(qscale[:, 0:1], arec[:, 0:1], 127.0, rms[:, :], ALU.mult, ALU.mult))

            def dequant_input(b):
                step = Steps(dve, in_step, b, 8)
                step.at = step.at + 7
                dve.wait_ge(gelu_done, b * 2)
                step.done(dve.tensor_scalar(dequant[:, 0:1], amax_c[:, 0:1], w_mean[:, 0:1], 1.0 / 127.0, ALU.mult, ALU.mult))

            def quant_input(b):
                step = Steps(dve, xq_step, b, 2)
                dve.wait_ge(xr_ready, b + 1)
                step.done(dve.tensor_scalar(xq[:, :], xr[:, :], ROUND, 127.0, ALU.subtract, ALU.min))

            def copy_input(b):
                step = Steps(dve, xq_step, b, 2)
                step.at = step.at + 1
                dve.wait_ge(xq_turned, b + 1)
                step.done(dve.tensor_scalar(xq_t[:, :, :].rearrange("p f q -> p (f q)"), ps_t_bf[:, 0:D], -128.0, None, ALU.max))

            def scale_hidden(b):
                step = Steps(dve, hid_step, b, 5)
                dve.wait_ge(gelu_done, b * 2 + 2)
                dve.wait_ge(hid_step, b * 5)
                step.done(dve.tensor_reduce(amax[:, 1:2], hid[:, :], AX.X, ALU.max, apply_absolute_value=True)).wait()
                step.done(dve.tensor_scalar(amax_c[:, 1:2], amax[:, 1:2], QEPS, None, ALU.max)).wait()
                step.done(dve.reciprocal(arec[:, 1:2], amax_c[:, 1:2])).wait()
                step.done(dve.tensor_scalar(qscale[:, 1:2], arec[:, 1:2], 127.0, None, ALU.mult))

            def quant_hidden(b):
                dve.wait_ge(hr_ready, b + 1)
                dve.tensor_scalar(hq[:, :], hr[:, :], ROUND, 127.0, ALU.subtract, ALU.min).then_inc(hq_ready, 1)

            def dequant_hidden(b):
                step = Steps(dve, hid_step, b, 5)
                dve.wait_ge(down_step, b * 2)
                step.at = step.at + 4
                step.done(dve.tensor_scalar(dequant[:, 1:2], amax_c[:, 1:2], w_mean[:, 1:2], 1.0 / 127.0, ALU.mult, ALU.mult))

            def copy_hidden(b):
                step = Steps(dve, down_step, b, 2)
                dve.wait_ge(hq_turned, b + 1)
                step.done(dve.tensor_scalar(hq_t[:, :, :].rearrange("p k q -> p (k q)"),
                                            ps_ut_bf.rearrange("p k q -> p (k q)"), -128.0, None, ALU.max))

            def add_output(b):
                step = Steps(dve, down_step, b, 2)
                step.at = step.at + 1
                dve.wait_ge(y_ready, b + 1)
                dve.wait_ge(hid_step, b * 5 + 5)
                dve.wait_ge(stored, b * 16)
                step.done(dve.scalar_tensor_tensor(out=y[:, :], in0=ps_ff[:, 0:D], scalar=dequant[:, 1:2], in1=stream(b),
                                                   op0=ALU.mult, op1=ALU.add))

            def mlp(t):
                if active(t, UP):
                    quant_input(t + UP)
                if active(t, SCALE_IN):
                    scale_input_stats(t + SCALE_IN)
                if active(t, UP):
                    copy_input(t + UP)
                if active(t, HIDDEN):
                    scale_hidden(t + HIDDEN)
                if active(t, DOWN):
                    copy_hidden(t + DOWN)
                if active(t, SCALE_IN):
                    scale_input_max(t + SCALE_IN)
                if active(t, HIDDEN):
                    quant_hidden(t + HIDDEN)
                if active(t, SCALE_IN):
                    scale_input(t + SCALE_IN)
                if active(t, DOWN):
                    add_output(t + DOWN)
                if active(t, HIDDEN):
                    dequant_hidden(t + HIDDEN)
                if active(t, SCALE_IN):
                    dequant_input(t + SCALE_IN)

            dve.wait_ge(t_read, STREAM_DONE)
            mlp_iterations(dve, mlp)


def kernel(**inputs):
    import numpy as np
    import concourse.bacc as bacc
    from concourse.bass_utils import run_bass_kernel_spmd

    a = {k: np.asarray(v) for k, v in inputs.items()}
    c = a["ctx_2048"]
    turned = c.reshape(NB, P, FT, P).transpose(0, 3, 2, 1).reshape(NB, P, D)
    lora_a = a["L0_ffn_lora_A"].transpose(1, 0, 2).reshape(D, ER)
    arrays = {
        "x": a["x"],
        "kv": np.stack([turned, c], axis=2),
        "w_ff": np.concatenate([a["L0_ffn_base_w"].T, lora_a, a["L0_ffn_router_w"].T], axis=1),
        "base_b": a["L0_ffn_base_b"],
        "router_b": a["L0_ffn_router_b"],
        "lora_b": a["L0_ffn_lora_B"].reshape(ER, D),
        "attn_gamma": a["L1_xattn_gamma"].reshape(1),
        "w1": a["L1_ffn_w1"].T,
        "w2": a["L1_ffn_w2"].T,
        "mlp_gamma": a["L1_ffn_gamma"],
    }
    nc = bacc.Bacc("TRN2", target_bir_lowering=False, num_devices=1)
    aps = {}
    for name, v in arrays.items():
        arrays[name] = v = np.ascontiguousarray(v)
        aps[name] = nc.dram_tensor(f"in_{name}", v.shape, mybir.dt.from_np(v.dtype), kind="ExternalInput").ap()
    out = nc.dram_tensor("out", (NB, P, D), F32, kind="ExternalOutput").ap()
    program(nc, out=out, **aps)
    r = run_bass_kernel_spmd(nc, [{f"in_{k}": v for k, v in arrays.items()}], core_ids=[0])
    return r.results[0]["out"]
```
